# Optimizing a Trainium2 kernel written in Bass

```python
import numpy as np
import jax
import jax.numpy as jnp

def _softmax(x, axis=-1):
    return jax.nn.softmax(x, axis=axis)

def _gelu(x):
    return jax.nn.gelu(x, approximate=True)

def _silu(x):
    return jax.nn.silu(x)

def _sigmoid(x):
    return jax.nn.sigmoid(x)

def _layernorm(x, axis=-1, eps=1e-05):
    m = jnp.mean(x, axis=axis, keepdims=True)
    v = jnp.var(x, axis=axis, keepdims=True)
    return (x - m) / jnp.sqrt(v + eps)

def _scatter_add(tgt, idx, src, axis=0):
    return tgt.at[idx].add(src)

def _segment_sum(src, seg, n):
    return jax.ops.segment_sum(src, seg, n)
kernel_name = 'mk_macaron_d1_jaxref_r8_c2b3c5'

def setup_inputs(seed: int=0):
    np.random.seed(seed)
    _w = jnp.asarray

    def _L0_attn_setup():
        import jax, jax.numpy as jnp
        import numpy as np
        EMBED_DIM = 128
        NUM_HEADS = 16
        HEAD_DIM = EMBED_DIM // NUM_HEADS
        key = jax.random.key(seed)
        ks = jax.random.split(key, 9)
        B, S, E = (2, 256, EMBED_DIM)
        scale = 1.0 / np.sqrt(E)
        inp = {'x': jax.random.normal(ks[0], (B, S, E), dtype=jnp.float32), 'Wq': jax.random.normal(ks[1], (E, E), dtype=jnp.float32) * scale, 'bq': jnp.zeros((E,), dtype=jnp.float32), 'Wk': jax.random.normal(ks[2], (E, E), dtype=jnp.float32) * scale, 'bk': jnp.zeros((E,), dtype=jnp.float32), 'Wv': jax.random.normal(ks[3], (E, E), dtype=jnp.float32) * scale, 'bv': jnp.zeros((E,), dtype=jnp.float32), 'Wo': jax.random.normal(ks[4], (E, E), dtype=jnp.float32) * scale, 'bo': jnp.zeros((E,), dtype=jnp.float32)}
        return inp
    _L0_attn_in = _L0_attn_setup()

    def _L0_ffn_setup():
        import jax, jax.numpy as jnp
        import numpy as np
        D_IN, D_HID = (128, 512)

        def _ternary(key, shape):
            return jax.random.randint(key, shape, -1, 2).astype(jnp.float32)

        def _tlin(x, w, s):
            return jnp.einsum('bsi,oi->bso', x, w) * s
        key = jax.random.key(seed)
        ks = jax.random.split(key, 12)
        inv = lambda fan: 1.0 / np.sqrt(fan).astype(np.float32)
        return {'x': jax.random.normal(ks[0], (4, 256, D_IN), dtype=jnp.float32), 'w1_w': _ternary(ks[1], (D_HID, D_IN)), 'w1_s': jax.random.uniform(ks[2], (D_HID,), dtype=jnp.float32) * inv(D_IN), 'w2_w': _ternary(ks[3], (D_HID, D_IN)), 'w2_s': jax.random.uniform(ks[4], (D_HID,), dtype=jnp.float32) * inv(D_IN), 'h1_w': _ternary(ks[5], (D_HID, D_HID)), 'h1_s': jax.random.uniform(ks[6], (D_HID,), dtype=jnp.float32) * inv(D_HID), 'h2_w': _ternary(ks[7], (D_HID, D_HID)), 'h2_s': jax.random.uniform(ks[8], (D_HID,), dtype=jnp.float32) * inv(D_HID), 'w3_w': _ternary(ks[9], (D_IN, D_HID)), 'w3_s': jax.random.uniform(ks[10], (D_IN,), dtype=jnp.float32) * inv(D_HID)}
    _L0_ffn_in = _L0_ffn_setup()
    _d = {'L0_attn_x': _L0_attn_in['x'], 'L0_attn_Wq': _L0_attn_in['Wq'], 'L0_attn_bq': _L0_attn_in['bq'], 'L0_attn_Wk': _L0_attn_in['Wk'], 'L0_attn_bk': _L0_attn_in['bk'], 'L0_attn_Wv': _L0_attn_in['Wv'], 'L0_attn_bv': _L0_attn_in['bv'], 'L0_attn_Wo': _L0_attn_in['Wo'], 'L0_attn_bo': _L0_attn_in['bo'], 'L0_ffn_w1_w': _L0_ffn_in['w1_w'], 'L0_ffn_w1_s': _L0_ffn_in['w1_s'], 'L0_ffn_w2_w': _L0_ffn_in['w2_w'], 'L0_ffn_w2_s': _L0_ffn_in['w2_s'], 'L0_ffn_h1_w': _L0_ffn_in['h1_w'], 'L0_ffn_h1_s': _L0_ffn_in['h1_s'], 'L0_ffn_h2_w': _L0_ffn_in['h2_w'], 'L0_ffn_h2_s': _L0_ffn_in['h2_s'], 'L0_ffn_w3_w': _L0_ffn_in['w3_w'], 'L0_ffn_w3_s': _L0_ffn_in['w3_s']}
    _x0 = _d['L0_attn_x']
    _d['L0_attn_x'] = jax.random.normal(jax.random.fold_in(jax.random.key(seed), 1), (16, 256, 128), dtype=_x0.dtype)
    del _x0
    return _d

def reference(L0_attn_x, L0_attn_Wq, L0_attn_bq, L0_attn_Wk, L0_attn_bk, L0_attn_Wv, L0_attn_bv, L0_attn_Wo, L0_attn_bo, L0_ffn_w1_w, L0_ffn_w1_s, L0_ffn_w2_w, L0_ffn_w2_s, L0_ffn_h1_w, L0_ffn_h1_s, L0_ffn_h2_w, L0_ffn_h2_s, L0_ffn_w3_w, L0_ffn_w3_s):

    def _L0_attn_ref(x, Wq, bq, Wk, bk, Wv, bv, Wo, bo):
        import jax, jax.numpy as jnp
        import numpy as np
        EMBED_DIM = 128
        NUM_HEADS = 16
        HEAD_DIM = EMBED_DIM // NUM_HEADS
        B, S, E = x.shape
        H, D = (NUM_HEADS, HEAD_DIM)
        sm_scale = D ** (-0.5)

        def proj(W, b):
            y = jnp.einsum('bse,fe->bsf', x, W) + b
            return y.reshape(B, S, H, D).transpose(0, 2, 1, 3)
        q = proj(Wq, bq)
        k = proj(Wk, bk)
        v = proj(Wv, bv)
        scores = jnp.einsum('bhqd,bhkd->bhqk', q, k) * sm_scale
        attn = jax.nn.softmax(scores, axis=-1)
        o = jnp.einsum('bhqk,bhkd->bhqd', attn, v)
        o = o.transpose(0, 2, 1, 3).reshape(B, S, E)
        return jnp.einsum('bse,fe->bsf', o, Wo) + bo

    def _L0_ffn_ref(x, w1_w, w1_s, w2_w, w2_s, h1_w, h1_s, h2_w, h2_s, w3_w, w3_s):
        import jax, jax.numpy as jnp
        import numpy as np
        D_IN, D_HID = (128, 512)

        def _ternary(key, shape):
            return jax.random.randint(key, shape, -1, 2).astype(jnp.float32)

        def _tlin(x, w, s):
            return jnp.einsum('bsi,oi->bso', x, w) * s
        h = jax.nn.silu(_tlin(x, w1_w, w1_s)) * _tlin(x, w2_w, w2_s)
        h = jax.nn.gelu(_tlin(h, h1_w, h1_s), approximate=False)
        h = jax.nn.gelu(_tlin(h, h2_w, h2_s), approximate=False)
        return _tlin(h, w3_w, w3_s)
    x = L0_attn_x
    x = x + 0.5 * _L0_ffn_ref(_layernorm(x, axis=-1), L0_ffn_w1_w, L0_ffn_w1_s, L0_ffn_w2_w, L0_ffn_w2_s, L0_ffn_h1_w, L0_ffn_h1_s, L0_ffn_h2_w, L0_ffn_h2_s, L0_ffn_w3_w, L0_ffn_w3_s)
    x = x + _L0_attn_ref(_layernorm(x, axis=-1), L0_attn_Wq, L0_attn_bq, L0_attn_Wk, L0_attn_bk, L0_attn_Wv, L0_attn_bv, L0_attn_Wo, L0_attn_bo)
    x = x + 0.5 * _L0_ffn_ref(_layernorm(x, axis=-1), L0_ffn_w1_w, L0_ffn_w1_s, L0_ffn_w2_w, L0_ffn_w2_s, L0_ffn_h1_w, L0_ffn_h1_s, L0_ffn_h2_w, L0_ffn_h2_s, L0_ffn_w3_w, L0_ffn_w3_s)
    return x

_drawn_inputs = setup_inputs


def setup_inputs(seed=0):
    import zlib

    import numpy as np

    out = dict(_drawn_inputs(seed))
    spreads = {'L0_attn_bq': (0.0, 0.1),
     'L0_attn_bk': (0.0, 0.1),
     'L0_attn_bv': (0.0, 0.1),
     'L0_attn_bo': (0.0, 0.1)}
    factors = {}
    for name, (base, spread) in spreads.items():
        noise = np.random.default_rng([zlib.crc32(name.encode()), seed]).standard_normal(out[name].shape)
        drawn = base * np.exp(spread * noise) if base else spread * noise
        out[name] = jnp.asarray(drawn.astype(out[name].dtype))
    for name, factor in factors.items():
        out[name] = (out[name] * factor).astype(out[name].dtype)
    return out
```

```python
from contextlib import ExitStack

import concourse.bass as bass
from concourse import mybir

F32 = mybir.dt.float32
F32R = mybir.dt.float32r
I32 = mybir.dt.int32
ALU = mybir.AluOpType
ACT = mybir.ActivationFunctionType
AX = mybir.AxisListType

P = 128
BANKS = 8
TOK = 512
TT = TOK // P
HT = 4
SLOTS = 4
EPS = 1e-5
RSQRT_MAGIC = 0x5F3759DF
NEWTON = 3
HEADS, HD = 16, 8
PAIRS = HEADS // 2
SEQ = 256
SCALE = HD ** -0.5
VW = HD + 1
VROW = 168
UNITS = 16
SKEW = 4
CREDIT = 2
W_CHUNKS = 11
C_W1, C_W2, C_H1, C_H2, C_W3 = 0, 1, 2, 6, 10


def macaron_kernel(nc, x, w_ffn, w_att, s12, sg, s3, bqk, bv, bo, eye, out):
    NT = x.shape[0] // P
    NB = NT // TT
    NP = NB // 2
    NBATCH = x.shape[0] // SEQ
    NPAIR = NBATCH // 2
    x_t = x.rearrange("(t p) d -> p t d", p=P)
    out_t = out.rearrange("(t p) d -> p t d", p=P)
    qk_scratch = nc.dram_tensor("qk_scratch", (2, P, 4, 2 * SEQ), F32).ap()

    ctx = ExitStack()
    with ctx:
        def sb(name, shape, dt=F32, c=ctx):
            return c.enter_context(nc.sbuf_tensor(name, shape, dt))

        def sem(name):
            return ctx.enter_context(nc.semaphore(name))

        bank = [ctx.enter_context(nc.psum_tensor(f"bank{i}", [P, 512], F32)) for i in range(BANKS)]
        X = sb("X", [P, NT, P])
        WH = sb("WH", [P, W_CHUNKS, 512], F32R)
        WL = sb("WL", [P, W_CHUNKS, 512], F32R)
        WA = sb("WA", [P, 4, P])
        S12 = sb("S12", [P, 2, HT])
        SG = sb("SG", [P, 2, HT])
        S3 = sb("S3", [P, 1])
        S3H = sb("S3H", [P, 1])
        BQK = sb("BQK", [P, 2])
        BV = sb("BV", [P, TT, P])
        BO = sb("BO", [1, P])
        EYE = sb("EYE", [P, P])
        ONES = sb("ONES", [P, P])
        stats = sb("stats", [P, 8, 6])
        moments = sb("moments", [P, 8, 2])
        var = sb("var", [P, 8])
        var_m = sb("var_m", [P, 8])
        C15 = sb("C15", [P, 8])
        scrap = sb("scrap", [P, 1])
        half = sb("half", [P, 8], I32)
        rstd = sb("rstd", [P, 8])
        newton = sb("newton", [P, 8])
        lo_max = sb("lo_max", [P, W_CHUNKS + 1])
        flag = sb("flag", [1, 1])
        xn = sb("xn", [P, 8, P])

        ffn = ExitStack()
        raw = sb("raw", [P, 3, 512], F32, ffn)
        x_hi = sb("x_hi", [P, 2, TOK], F32R, ffn)
        x_lo = sb("x_lo", [P, 2, TOK], F32R, ffn)
        act_hi = [sb(f"act{n}_hi", [P, 2, HT, TOK], F32R, ffn) for n in range(3)]
        act_lo = [sb(f"act{n}_lo", [P, 2, HT, TOK], F32R, ffn) for n in range(3)]
        silu = sb("silu", [P, SLOTS, TOK], F32, ffn)
        full = sb("full", [P, SLOTS, TOK], F32, ffn)
        yT = sb("yT", [P, 2, TOK], F32, ffn)
        ffn.close()
        att = ExitStack()
        QA = [sb(f"QA{i}", [P, PAIRS, 2 * SEQ], F32R, att) for i in range(2)]
        KA = [sb(f"KA{i}", [P, HEADS, 2 * SEQ], F32R, att) for i in range(2)]
        V = [sb(f"V{i}", [P, TT, VROW], F32, att) for i in range(2)]
        probs = sb("probs", [P, 8, 2 * SEQ], F32, att)
        xT = sb("xT", [P, 2 * SEQ], F32, att)
        qk = sb("qk", [P, 4, 2 * SEQ], F32R, att)
        oT = sb("oT", [P, 4, SEQ], F32, att)
        o_sum = sb("o_sum", [P, 2, HEADS], F32, att)
        o_nat = sb("o_nat", [P, 2, P], F32, att)
        onT = sb("onT", [P, SEQ], F32, att)
        neg_max = sb("neg_max", [P, 2, HEADS], F32, att)
        m_parts = sb("m_parts", [HEADS, 2, SEQ], F32R, att)
        att.close()

        consts_in = sem("consts_in")
        x_in = sem("x_in")
        w_in = [sem(f"w_in{i}") for i in range(3)]
        ones_set = sem("ones_set")
        c15_set = sem("c15_set")
        s3_half = sem("s3_half")
        w_hi = sem("w_hi")
        w_lo = sem("w_lo")
        lo_reduced = sem("lo_reduced")
        flag_sum = sem("flag_sum")
        flag_set = sem("flag_set")
        stats_done = sem("stats_done")
        moments_done = sem("moments_done")
        var_done = sem("var_done")
        half_done = sem("half_done")
        guess_done = sem("guess_done")
        rstd_done = sem("rstd_done")
        newton_step = sem("newton_step")
        xn_done = sem("xn_done")
        xT_done = sem("xT_done")
        xhi_done = sem("xhi_done")
        xlo_done = sem("xlo_done")
        gate_mm = sem("gate_mm")
        up_mm = sem("up_mm")
        silu_done = sem("silu_done")
        h_full = sem("h_full")
        h_hi = sem("h_hi")
        h_lo = sem("h_lo")
        hid_mm = sem("hid_mm")
        g_hi = sem("g_hi")
        g_lo = sem("g_lo")
        out_mm = sem("out_mm")
        y_scaled = sem("y_scaled")
        y_back = sem("y_back")
        x_added = sem("x_added")
        stored = sem("stored")
        pads_set = sem("pads_set")
        qa_cleared = sem("qa_cleared")
        a_xT = sem("a_xT")
        a_xT_sb = sem("a_xT_sb")
        q_mm = sem("q_mm")
        k_mm = sem("k_mm")
        v_mm = sem("v_mm")
        q_hi = sem("q_hi")
        q_lo = sem("q_lo")
        k_hi = sem("k_hi")
        k_lo = sem("k_lo")
        v_set = sem("v_set")
        qk_written = sem("qk_written")
        qk_loaded = sem("qk_loaded")
        a_mm = sem("a_mm")
        max_done = sem("max_done")
        m_T = sem("m_T")
        m_hi = sem("m_hi")
        m_lo = sem("m_lo")
        m_loaded = sem("m_loaded")
        b_mm = sem("b_mm")
        exp_done = sem("exp_done")
        pv_mm = sem("pv_mm")
        o_out = sem("o_out")
        o_tok = sem("o_tok")
        sums_inv = sem("sums_inv")
        o_norm = sem("o_norm")
        on_T = sem("on_T")
        on_T_sb = sem("on_T_sb")
        y_mm = sem("y_mm")
        att_added = sem("att_added")

        N_CONSTS = 11
        PADS = 5
        L1_TILES = HT * 2
        HID_TILES = HT * 4

        block = ctx.enter_context(nc.Block())

        def wait(eng, s, v):
            if not isinstance(v, int) or v > 0:
                eng.wait_ge(s, v)

        def ffn_is_over(eng, f):
            eng.wait_ge(x_added, NB * (f + 1) + CREDIT)

        def att_is_over(eng):
            eng.wait_ge(att_added, NBATCH)

        @block.sync
        def _(sp):
            def weights(c):
                if c >= 3:
                    sp.wait_ge(w_lo, c - 2)
                sp.dma_start(raw[:, c % 3, :], w_ffn[:, c, :]).then_inc(w_in[c % 3], 16)

            def load_x(i):
                sp.dma_start(X[:, 8 * i:8 * i + 8, :], x_t[:, 8 * i:8 * i + 8, :]).then_inc(x_in, 16)

            load_x(0)
            weights(0)
            weights(1)
            for dst, src in ((EYE[:, :], eye), (S12[:, :, :], s12), (SG[:, :, :], sg), (S3[:, :], s3),
                             (BQK[:, :], bqk), (BO[:, :], bo), (WA[:, :, :], w_att)):
                sp.dma_start(dst, src).then_inc(consts_in, 16)
            for t in range(TT):
                sp.dma_start(BV[:, t, :], bv.partition_broadcast(P)).then_inc(consts_in, 16)
            weights(2)
            for c in range(3, W_CHUNKS):
                weights(c)
                if c % 3 == 0:
                    load_x(c // 3)

            def place_qk(q, par):
                for c, lo in ((0, q_lo), (2, k_lo)):
                    sp.wait_ge(lo, q + 1)
                    sp.dma_start(qk_scratch[par][:, c:c + 2, :], qk[:, c:c + 2, :].bitcast(F32))\
                      .then_inc(qk_written, 16)
                sp.wait_ge(qk_written, 32 * q + 32)
                src = qk_scratch[par].rearrange("(hp s d) c t -> s c d hp t", s=2, d=HD)
                for s in range(2):
                    for r in range(4):
                        row = 64 * s + HD * r
                        sp.dma_start(QA[par][row:row + HD, :, :].bitcast(F32), src[s, r % 2])\
                          .then_inc(qk_loaded, 16)
                        sp.dma_start(KA[par][row:row + HD, s:HEADS:2, :].bitcast(F32), src[s, 2 + r // 2])\
                          .then_inc(qk_loaded, 16)

            def place_max(b, par, bb):
                sp.wait_ge(m_lo, b + 1)
                for s in range(2):
                    for c in range(2):
                        row = 64 * s + 32 + c
                        sp.dma_start(QA[par][row:row + 1, :, SEQ * bb:SEQ * bb + SEQ].bitcast(F32),
                                     m_parts[s:HEADS:2, c, :].bitcast(F32)).then_inc(m_loaded, 16)

            sp.wait_ge(pads_set, PADS)
            place_qk(0, 0)
            place_max(0, 0, 0)

            def att_body(i, par, project=True, more=True, clear=True):
                if project:
                    place_qk(i + 1, 1 - par)
                place_max(2 * i + 1, par, 1)
                if more:
                    place_max(2 * i + 2, 1 - par, 0)
                if clear:
                    sp.wait_ge(b_mm, 2 * UNITS * (i + 1))
                    for s in range(2):
                        row = 64 * s + 32
                        sp.dma_start(QA[par][row:row + 2, :, :].bitcast(F32),
                                     KA[par][row + 2:row + 4, s:HEADS:2, :].bitcast(F32))\
                          .then_inc(qa_cleared, 16)

            sp.wait_ge(pads_set, 2 * PADS)
            att_body(0, 0)
            att_body(1, 1)
            with sp.Fori(1, NPAIR // 2 - 1) as n:
                att_body(2 * n, 0)
                att_body(2 * n + 1, 1)
            att_body(NPAIR - 2, 0, clear=False)
            att_body(NPAIR - 1, 1, project=False, more=False, clear=False)

            with sp.Fori(0, NP) as i:
                sp.wait_ge(x_added, NB + 2 * i + 2 + CREDIT)
                sp.dma_start(out_t[:, bass.ds(8 * i, 8), :], X[:, bass.ds(8 * i, 8), :]).then_inc(stored, 16)
            sp.wait_ge(stored, 16 * NP)

        @block.gpsimd
        def _(pool):
            pool.memset(C15[:, :], 1.5).then_inc(c15_set, 1)
            pool.memset(ONES[:, :], 1.0).then_inc(ones_set, 1)
            pool.wait_ge(c15_set, 1)

            def rsqrt_steps(n, base, width=8):
                pool.wait_ge(guess_done, n + 1)
                v, y, a = var_m[:, 0:width], rstd[:, 0:width], newton[:, 0:width]
                k = 0
                for it in range(NEWTON):
                    last = it == NEWTON - 1
                    for step in range(4):
                        if step == 0:
                            ins = pool.tensor_tensor(a, y, y, op=ALU.mult)
                        elif step == 1:
                            ins = pool.tensor_tensor(a, a, v, op=ALU.mult)
                        elif step == 2:
                            ins = pool.tensor_tensor(a, a, C15[:, 0:width], op=ALU.add)
                        else:
                            ins = pool.tensor_tensor(y, y, a, op=ALU.mult)
                        if last and step == 3:
                            ins.then_inc(rstd_done, 1)
                        else:
                            k += 1
                            ins.then_inc(newton_step, 1)
                            pool.wait_ge(newton_step, base + k)

            K = 4 * NEWTON - 1

            def ffn_norms(f):
                n0 = f * (NP + NPAIR)
                rsqrt_steps(n0, K * n0)
                with pool.Fori(1, NP) as i:
                    rsqrt_steps(n0 + i, K * (n0 + i))

            ffn_norms(0)
            ffn_is_over(pool, 0)
            for par in range(2):
                if par == 1:
                    rsqrt_steps(NP, K * NP, 4)
                    pool.wait_ge(rstd_done, NP + 1)
                n = PADS * par
                for s in range(2):
                    pool.memset(QA[par][64 * s + 32:64 * s + 64, :, :].bitcast(F32), 0.0).then_inc(pads_set, 1)
                    pool.wait_ge(pads_set, n + s + 1)
                pool.memset(KA[par][:, :, :].bitcast(F32), 0.0).then_inc(pads_set, 1)
                for s in range(2):
                    pool.wait_ge(pads_set, n + s + 3)
                    pool.memset(KA[par][64 * s + 32:64 * s + 34, s:HEADS:2, :].bitcast(F32), 1.0)\
                        .then_inc(pads_set, 1)
                pool.wait_ge(pads_set, n + PADS)
            rsqrt_steps(NP + 1, K * (NP + 1), 4)

            with pool.Fori(0, NPAIR - 2) as i:
                rsqrt_steps(NP + i + 2, K * (NP + i + 2), 4)
            ffn_norms(1)

        @block.scalar
        def _(act):
            A = nc.scalar
            A.sem_inc(g_hi, CREDIT)
            A.sem_inc(exp_done, CREDIT)
            A.sem_inc(o_out, CREDIT)

            def weight_hi(c):
                act.wait_ge(w_in[c % 3], 16 * (c // 3 + 1))
                A.activation(WH[:, c, :], raw[:, c % 3, :], ACT.Copy).then_inc(w_hi, 1)

            def split_x(n, j):
                act.wait_ge(xT_done, n + 1)
                A.activation(x_hi[:, j, :], bank[6 + j][:, :], ACT.Copy).then_inc(xhi_done, 1)

            def layer1(n0, j):
                def hi(t):
                    act.wait_ge(h_full, n0 + t + 1)
                    A.activation(act_hi[0][:, j, t, :], silu[:, t, :], ACT.Copy).then_inc(h_hi, 1)
                for t in range(HT):
                    n = n0 + t
                    act.wait_ge(gate_mm, n + 1)
                    wait(act, h_lo, n - SLOTS + 1)
                    A.activation(silu[:, t, :], bank[t % 2][:, :], ACT.Silu,
                                 scale=S12[:, 0, t:t + 1]).then_inc(silu_done, 1)
                    if t >= 1:
                        hi(t - 1)
                hi(HT - 1)

            def hidden(n0, layer, j):
                for t in range(HT):
                    n = n0 + t
                    act.wait_ge(hid_mm, n + 1)
                    act.wait_ge(g_lo, n + 1)
                    A.activation(full[:, t, :], bank[4 + t % 2][:, :], ACT.Gelu,
                                 scale=SG[:, layer, t:t + 1])
                    A.activation(act_hi[1 + layer][:, j, t, :], bank[4 + t % 2][:, :], ACT.Gelu,
                                 scale=SG[:, layer, t:t + 1]).then_inc(g_hi, 1)

            def output(n, j):
                act.wait_ge(out_mm, n + 1)
                A.activation(yT[:, j, :], bank[6 + j][:, :], ACT.Copy, scale=S3H[:, 0:1]).then_inc(y_scaled, 1)

            def ffn_phase(f):
                t1, t2, nb = f * NB * HT, f * NP * HID_TILES, f * NB

                def body(i, more=True):
                    g = t2 + HID_TILES * i
                    hidden(g, 0, 0)
                    hidden(g + HT, 0, 1)
                    if more:
                        split_x(nb + 2 * i + 2, 0)
                        split_x(nb + 2 * i + 3, 1)
                    hidden(g + 2 * HT, 1, 0)
                    hidden(g + 3 * HT, 1, 1)
                    if more:
                        layer1(t1 + L1_TILES * (i + 1), 0)
                    output(nb + 2 * i, 0)
                    output(nb + 2 * i + 1, 1)
                    if more:
                        layer1(t1 + L1_TILES * (i + 1) + HT, 1)

                if f == 0:
                    weight_hi(0)
                    weight_hi(1)
                split_x(nb, 0)
                if f == 0:
                    for c in range(2, 5):
                        weight_hi(c)
                split_x(nb + 1, 1)
                layer1(t1, 0)
                if f == 0:
                    act.wait_ge(s3_half, 1)
                    for c in range(5, W_CHUNKS):
                        weight_hi(c)
                layer1(t1 + HT, 1)
                with act.Fori(0, NP - 1) as i:
                    body(i)
                body(NP - 1, more=False)

            act.wait_ge(consts_in, 16 * N_CONSTS)
            ffn_phase(0)
            ffn_is_over(act, 0)

            def project_in(q):
                act.wait_ge(a_xT, q + 1)
                A.activation(xT[:, :], bank[6][:, :], ACT.Copy).then_inc(a_xT_sb, 1)
                for c, mm, done, b in ((0, q_mm, q_hi, 7), (2, k_mm, k_hi, 6)):
                    act.wait_ge(mm, q + 1)
                    if c == 0:
                        wait(act, qk_written, 32 * q)
                    A.activation(qk[:, c, :], bank[b][:, :], ACT.Identity, bias=BQK[:, c // 2:c // 2 + 1])\
                        .then_inc(done, 1)

            def exp_unit(b, u):
                n = UNITS * b + u
                act.wait_ge(b_mm, n + 1)
                act.wait_ge(pv_mm, 4 * b + u // 4 - 2 + 1 + CREDIT)
                A.activation(probs[:, u % 8, :], bank[2 + u % 2][:, :], ACT.Exp, scale=SCALE)\
                    .then_inc(exp_done, 1)

            def evacuate_o(b, g):
                act.wait_ge(pv_mm, 4 * b + g + 1 + CREDIT)
                A.activation(oT[:, g, :], bank[4 + g % 2][:, 0:SEQ], ACT.Copy).then_inc(o_out, 1)

            def split_max(b):
                act.wait_ge(m_T, b + 1)
                wait(act, m_loaded, 64 * b)
                A.activation(m_parts[:, 0, :], bank[7][0:HEADS, 0:SEQ], ACT.Copy).then_inc(m_hi, 1)

            def attend(b, more=True, before=True):
                for u in range(UNITS + SKEW):
                    if u == 3 and before:
                        act.wait_ge(on_T, b)
                        A.activation(onT[:, :], bank[6][:, 0:SEQ], ACT.Copy).then_inc(on_T_sb, 1)
                    if u >= SKEW:
                        exp_unit(b, u - SKEW)
                        v = u - SKEW
                        if v >= 6 and (v - 6) % 4 == 0:
                            evacuate_o(b, (v - 6) // 4)
                    if u == UNITS + 1 and more:
                        split_max(b + 1)
                evacuate_o(b, 3)

            project_in(0)
            split_max(0)

            def att_body(i, project=True, more=True, first=False):
                if project:
                    project_in(i + 1)
                attend(2 * i, before=not first)
                attend(2 * i + 1, more=more)

            att_body(0, first=True)
            att_body(1)
            with act.Fori(1, NPAIR // 2 - 1) as n:
                att_body(2 * n)
                att_body(2 * n + 1)
            att_body(NPAIR - 2)
            att_body(NPAIR - 1, project=False, more=False)
            act.wait_ge(on_T, NBATCH)
            A.activation(onT[:, :], bank[6][:, 0:SEQ], ACT.Copy).then_inc(on_T_sb, 1)
            att_is_over(act)
            ffn_phase(1)

        @block.vector
        def _(dve):
            D = nc.vector
            D.sem_inc(g_lo, SLOTS)
            D.sem_inc(x_added, CREDIT)

            def weight_lo(c):
                dve.wait_ge(w_hi, c + 1)
                D.tensor_tensor(WL[:, c, :], raw[:, c % 3, :], WH[:, c, :].bitcast(F32), op=ALU.subtract)\
                    .then_inc(w_lo, 1)

            def weight_lo_max(c):
                dve.wait_ge(w_lo, c + 1)
                D.tensor_reduce(lo_max[:, c:c + 1], WL[:, c, :].bitcast(F32), axis=AX.X, op=ALU.max,
                                apply_absolute_value=True).then_inc(lo_reduced, 1)

            def norm_steps(n, tile0, width=8):
                def s_stats():
                    for t in range(width):
                        ins = D.bn_stats(stats[:, t, :], X[:, bass.ds(tile0 + t, 1), :])
                    ins.then_inc(stats_done, 1)

                def s_moments():
                    dve.wait_ge(stats_done, n + 1)
                    D.memset(scrap[:, 0:1], 0.0)
                    for t in range(width):
                        ins = D.bn_aggr(moments[:, t, :], stats[:, t, :])
                    ins.then_inc(moments_done, 1)

                def s_var():
                    dve.wait_ge(moments_done, n + 1)
                    D.tensor_scalar(var_m[:, 0:width], moments[:, 0:width, 1], EPS, -0.5, ALU.add, ALU.mult)
                    D.tensor_scalar(var[:, 0:width], moments[:, 0:width, 1], EPS, None, ALU.add)\
                        .then_inc(var_done, 1)

                def s_half():
                    dve.wait_ge(var_done, n + 1)
                    D.tensor_scalar(half[:, 0:width], var[:, 0:width].bitcast(I32), 1, None,
                                    ALU.arith_shift_right).then_inc(half_done, 1)

                def s_guess():
                    dve.wait_ge(half_done, n + 1)
                    D.tensor_scalar(rstd[:, 0:width].bitcast(I32), half[:, 0:width], -1.0,
                                    float(RSQRT_MAGIC), ALU.mult, ALU.add).then_inc(guess_done, 1)

                return [s_stats, s_moments, s_var, s_half, s_guess]

            def normalise(n, tile0, t0, width=4):
                dve.wait_ge(rstd_done, n + 1)
                for t in range(t0, t0 + width):
                    ins = D.tensor_scalar(xn[:, t:t + 1, :], X[:, bass.ds(tile0 + t, 1), :],
                                          moments[:, t, 0:1], rstd[:, t:t + 1], ALU.subtract, ALU.mult)
                ins.then_inc(xn_done, 1)

            def low_x(n, j):
                dve.wait_ge(xhi_done, n + 1)
                D.tensor_tensor(x_lo[:, j, :], bank[6 + j][:, :], x_hi[:, j, :].bitcast(F32), op=ALU.subtract)\
                    .then_inc(xlo_done, 1)

            def layer1(n0, j):
                def lo(t):
                    dve.wait_ge(h_hi, n0 + t + 1)
                    D.tensor_tensor(act_lo[0][:, j, t, :], silu[:, t, :], act_hi[0][:, j, t, :].bitcast(F32),
                                    op=ALU.subtract).then_inc(h_lo, 1)
                for t in range(HT):
                    n = n0 + t
                    dve.wait_ge(silu_done, n + 1)
                    dve.wait_ge(up_mm, n + 1)
                    D.scalar_tensor_tensor(out=silu[:, t, :], in0=bank[2 + t % 2][:, :],
                                           scalar=S12[:, 1, t:t + 1], in1=silu[:, t, :],
                                           op0=ALU.mult, op1=ALU.mult).then_inc(h_full, 1)
                    if t >= 1:
                        lo(t - 1)
                lo(HT - 1)

            def hidden(n0, layer, j, between=()):
                for t in range(HT):
                    dve.wait_ge(g_hi, n0 + t + 1 + CREDIT)
                    D.tensor_tensor(act_lo[1 + layer][:, j, t, :], full[:, t, :],
                                    act_hi[1 + layer][:, j, t, :].bitcast(F32), op=ALU.subtract)\
                        .then_inc(g_lo, 1)
                    for step in between[t:t + 1]:
                        step()

            def residual(n, tile0, j):
                dve.wait_ge(y_back, n + 1)
                xs = X[:, bass.ds(tile0, TT), :]
                D.tensor_tensor(xs, bank[6 + j][:, :].rearrange("p (t d) -> p t d", t=TT), xs, op=ALU.add)\
                    .then_inc(x_added, 1)

            def ffn_phase(f):
                t1, t2, nb, n0 = f * NB * HT, f * NP * HID_TILES, f * NB, f * (NP + NPAIR)
                xn0 = f * (NB + NPAIR)

                def body(i, more=True):
                    g = t2 + HID_TILES * i
                    n, tile0 = n0 + i + 1, 8 * i + 8
                    if more:
                        if f == 0:
                            dve.wait_ge(x_in, 16 * i + 32)
                        steps = norm_steps(n, tile0)
                        steps[0]()
                        hidden(g, 0, 0, steps[1:])
                    else:
                        hidden(g, 0, 0)
                    hidden(g + HT, 0, 1)
                    if more:
                        normalise(n, tile0, 0)
                        normalise(n, tile0, 4)
                    hidden(g + 2 * HT, 1, 0)
                    if more:
                        low_x(nb + 2 * i + 2, 0)
                        low_x(nb + 2 * i + 3, 1)
                    hidden(g + 3 * HT, 1, 1)
                    if more:
                        layer1(t1 + L1_TILES * (i + 1), 0)
                        layer1(t1 + L1_TILES * (i + 1) + HT, 1)
                    residual(nb + 2 * i, 8 * i, 0)
                    residual(nb + 2 * i + 1, 8 * i + 4, 1)

                if f == 0:
                    dve.wait_ge(x_in, 16)
                for step in norm_steps(n0, 0):
                    step()
                if f == 0:
                    weight_lo(0)
                    weight_lo(1)
                normalise(n0, 0, 0)
                normalise(n0, 0, 4)
                low_x(nb, 0)
                if f == 0:
                    for c in range(2, 5):
                        weight_lo(c)
                low_x(nb + 1, 1)
                if f == 0:
                    dve.wait_ge(consts_in, 16 * N_CONSTS)
                    D.tensor_scalar(S3H[:, :], S3[:, :], 0.5, None, ALU.mult).then_inc(s3_half, 1)
                layer1(t1, 0)
                if f == 0:
                    for c in range(5, W_CHUNKS):
                        weight_lo(c)
                        weight_lo_max(c - 1)
                    for c in (0, 1, 2, 3, W_CHUNKS - 1):
                        weight_lo_max(c)
                    dve.wait_ge(lo_reduced, W_CHUNKS)
                    D.tensor_reduce(lo_max[:, W_CHUNKS:W_CHUNKS + 1], lo_max[:, 0:W_CHUNKS], axis=AX.X,
                                    op=ALU.max).then_inc(lo_reduced, 1)
                layer1(t1 + HT, 1)
                if f == 0:
                    dve.wait_ge(flag_sum, 1)
                    D.tensor_copy(flag[:, :], bank[4][0:1, 0:1]).then_inc(flag_set, 1)
                with dve.Fori(0, NP - 1) as i:
                    body(i)
                body(NP - 1, more=False)

            ffn_phase(0)

            for par in range(2):
                D.memset(V[par][:, :, :], 0.0).then_inc(v_set, 1)
            dve.wait_ge(v_set, 2)
            for par in range(2):
                D.memset(V[par][:, :, 0:HEADS * VW].rearrange("p t (h v) -> p t h v", v=VW)[:, :, :, HD:VW], 1.0)\
                    .then_inc(v_set, 1)

            def project_in(q, par):
                for c, hi, lo, b in ((0, q_hi, q_lo, 7), (2, k_hi, k_lo, 6)):
                    dve.wait_ge(hi, q + 1)
                    D.scalar_tensor_tensor(out=qk[:, c + 1, :], in0=bank[b][:, :],
                                           scalar=BQK[:, c // 2:c // 2 + 1], in1=qk[:, c, :].bitcast(F32),
                                           op0=ALU.add, op1=ALU.subtract).then_inc(lo, 1)
                dve.wait_ge(v_mm, q + 1)
                for t in range(TT):
                    ins = D.tensor_tensor(
                        V[par][:, t, 0:HEADS * VW].rearrange("p (h v) -> p h v", v=VW)[:, :, 0:HD],
                        bank[7][:, P * t:P * t + P].rearrange("p (h v) -> p h v", v=HD),
                        BV[:, t, :].rearrange("p (h v) -> p h v", v=HD), op=ALU.add)
                ins.then_inc(v_set, 1)

            def max_unit(b, u):
                dve.wait_ge(a_mm, UNITS * b + u + 1)
                qt, hp = u // PAIRS, u % PAIRS
                D.tensor_reduce(neg_max[:, qt, 2 * hp:2 * hp + 2],
                                bank[u % 2][:, :].rearrange("p (h k) -> p h k", h=2), axis=AX.X,
                                op=ALU.max, negate=True).then_inc(max_done, 1)

            def low_max(b):
                dve.wait_ge(m_hi, b + 1)
                D.tensor_tensor(m_parts[:, 1, :], bank[7][0:HEADS, 0:SEQ], m_parts[:, 0, :].bitcast(F32),
                                op=ALU.subtract).then_inc(m_lo, 1)

            def o_of(qt):
                return bank[6 + qt][:, :].rearrange("p (h v) -> p h v", v=32)

            def norm_o(b, qt):
                dve.wait_ge(o_tok, 2 * b + qt + 1)
                D.reciprocal(o_sum[:, qt, :], o_of(qt)[:, :, HD]).then_inc(sums_inv, 1)

            def scale_o(b, qt):
                dve.wait_ge(sums_inv, 2 * b + qt + 1)
                D.tensor_tensor(o_nat[:, qt, :].rearrange("p (h v) -> p h v", v=HD), o_of(qt)[:, :, 0:HD],
                                o_sum[:, qt, :].unsqueeze(2).broadcast_to([P, HEADS, HD]), op=ALU.mult)\
                    .then_inc(o_norm, 1)

            def add_att(b, tile0):
                dve.wait_ge(y_mm, b + 1)
                xs = X[:, bass.ds(tile0, 2), :]
                D.tensor_tensor(xs, bank[7][:, 0:SEQ].rearrange("p (t d) -> p t d", t=2), xs, op=ALU.add)\
                    .then_inc(att_added, 1)

            def attend(b, more=True, before=True, norm=()):
                for u in range(UNITS + SKEW):
                    if u == 1 and before:
                        norm_o(b - 1, 0)
                        norm_o(b - 1, 1)
                        scale_o(b - 1, 0)
                        scale_o(b - 1, 1)
                    if u == 9 and before:
                        add_att(b - 1, 2 * b - 2)
                    if more and u < UNITS:
                        max_unit(b + 1, u)
                    if u >= 10:
                        for step in norm[u - 10:u - 9]:
                            step()
                    if u == UNITS + 1 and more:
                        low_max(b + 1)

            def norm_pair(q):
                return norm_steps(NP + q, 4 * q, 4)

            for step in norm_pair(0):
                step()
            normalise(NP, 0, 0)
            for step in norm_pair(1):
                step()
            project_in(0, 0)
            normalise(NP + 1, 4, 0)
            for u in range(UNITS):
                max_unit(0, u)
            low_max(0)

            def att_body(i, par, project=True, more=True, norm=True, first=False):
                if project:
                    project_in(i + 1, 1 - par)
                attend(2 * i, before=not first)
                attend(2 * i + 1, more=more, norm=norm_pair(i + 2) if norm else ())
                if norm:
                    normalise(NP + i + 2, 4 * i + 8, 0)

            att_body(0, 0, first=True)
            att_body(1, 1)
            with dve.Fori(1, NPAIR // 2 - 1) as n:
                att_body(2 * n, 0)
                att_body(2 * n + 1, 1)
            att_body(NPAIR - 2, 0, norm=False)
            att_body(NPAIR - 1, 1, project=False, more=False, norm=False)
            for f_ in (norm_o, scale_o):
                for qt in range(2):
                    f_(NBATCH - 1, qt)
            add_att(NBATCH - 1, 2 * NBATCH - 2)
            dve.wait_ge(att_added, NBATCH)
            ffn_phase(1)

        @block.tensor
        def _(pe):
            T = nc.tensor
            T.sem_inc(pv_mm, CREDIT)
            MM = T.matmul

            def split_mm(dst, w, xs, general):
                todo = [(wh, part) for (wh, _), (xh, xl) in zip(w, xs) for part in (xh, xl)]
                if general:
                    todo += [(wl, part) for (_, wl), (xh, xl) in zip(w, xs) for part in (xh, xl)]
                for k, (a, b) in enumerate(todo):
                    ins = MM(dst, a, b, start=k == 0, stop=k == len(todo) - 1)
                return ins

            def w_of(c, t):
                return WH[:, c, P * t:P * t + P], WL[:, c, P * t:P * t + P]

            def layer1(n0, nblk, j, general):
                pe.wait_ge(xlo_done, nblk + 1)
                xs = [(x_hi[:, j, :], x_lo[:, j, :])]
                for t in range(HT):
                    n = n0 + t
                    wait(pe, silu_done, n - 1)
                    split_mm(bank[t % 2][:, :], [w_of(C_W1, t)], xs, general).then_inc(gate_mm, 1)
                    wait(pe, h_full, n - 1)
                    split_mm(bank[2 + t % 2][:, :], [w_of(C_W2, t)], xs, general).then_inc(up_mm, 1)

            def inputs_of(layer, j):
                return [(act_hi[layer][:, j, k, :], act_lo[layer][:, j, k, :]) for k in range(HT)]

            def hidden(n0, layer, j, ready_sem, ready, general):
                pe.wait_ge(ready_sem, ready)
                xs = inputs_of(layer, j)
                c0 = (C_H1, C_H2)[layer]
                for t in range(HT):
                    pe.wait_ge(g_hi, n0 + t + 1)
                    split_mm(bank[4 + t % 2][:, :], [w_of(c0 + k, t) for k in range(HT)], xs, general)\
                        .then_inc(hid_mm, 1)

            def output(nblk, j, g_ready, general):
                pe.wait_ge(g_lo, g_ready + SLOTS)
                split_mm(bank[6 + j][:, :], [w_of(C_W3, k) for k in range(HT)], inputs_of(2, j), general)\
                    .then_inc(out_mm, 1)

            def transpose_x(nx, j):
                pe.wait_ge(xn_done, nx + 1)
                for t in range(TT):
                    ins = T.transpose(bank[6 + j][:, P * t:P * t + P], xn[:, 4 * j + t, :], EYE[:, :])
                ins.then_inc(xT_done, 1)

            def transpose_y(nblk, j):
                pe.wait_ge(y_scaled, nblk + 1)
                for t in range(TT):
                    ins = T.transpose(bank[6 + j][:, P * t:P * t + P], yT[:, j, P * t:P * t + P], EYE[:, :])
                ins.then_inc(y_back, 1)

            def ffn_bodies(f, general):
                t1, t2, nb, nx = f * NB * HT, f * NP * HID_TILES, f * NB, f * (NB + NPAIR)

                def body(i, more=True):
                    g = t2 + HID_TILES * i
                    hl = t1 + L1_TILES * i
                    hidden(g, 0, 0, h_lo, hl + HT, general)
                    hidden(g + HT, 0, 1, h_lo, hl + 2 * HT, general)
                    if more:
                        for j in range(2):
                            pe.wait_ge(x_added, nb + 2 * i - 1 + j + CREDIT)
                            transpose_x(nx + 2 * i + 2 + j, j)
                    hidden(g + 2 * HT, 1, 0, g_lo, g + HT + SLOTS, general)
                    hidden(g + 3 * HT, 1, 1, g_lo, g + 2 * HT + SLOTS, general)
                    if more:
                        layer1(hl + L1_TILES, nb + 2 * i + 2, 0, general)
                        pe.wait_ge(xlo_done, nb + 2 * i + 4)
                    else:
                        pe.wait_ge(x_added, nb + 2 * i + CREDIT)
                    output(nb + 2 * i, 0, g + 3 * HT, general)
                    output(nb + 2 * i + 1, 1, g + 4 * HT, general)
                    if more:
                        layer1(hl + L1_TILES + HT, nb + 2 * i + 3, 1, general)
                    transpose_y(nb + 2 * i, 0)
                    transpose_y(nb + 2 * i + 1, 1)

                if f == 1:
                    layer1(t1, nb, 0, general)
                    layer1(t1 + HT, nb + 1, 1, general)
                with pe.Fori(0, NP - 1) as i:
                    body(i)
                body(NP - 1, more=False)

            def ffn_phase(f, low_weights):
                t1, nb, nx = f * NB * HT, f * NB, f * (NB + NPAIR)
                if f == 0:
                    pe.wait_ge(consts_in, 16 * N_CONSTS)
                transpose_x(nx, 0)
                transpose_x(nx + 1, 1)
                if f == 0:
                    pe.wait_ge(w_lo, 2)
                if f == 0:
                    layer1(t1, nb, 0, True)
                    layer1(t1 + HT, nb + 1, 1, True)
                    pe.wait_ge(ones_set, 1)
                    pe.wait_ge(lo_reduced, W_CHUNKS + 1)
                    MM(bank[4][0:1, 0:1], ONES[:, 0:1], lo_max[:, W_CHUNKS:W_CHUNKS + 1],
                       start=True, stop=True).then_inc(flag_sum, 1)
                    pe.wait_ge(flag_set, 1)
                    pe.reg_load(low_weights, flag[0:1, 0:1].bitcast(I32))
                with pe.If_ne(low_weights, 0):
                    ffn_bodies(f, True)
                with pe.Else():
                    ffn_bodies(f, False)

            low_weights = T.alloc_register("low_weights")
            ffn_phase(0, low_weights)
            ffn_is_over(pe, 0)

            def project_in(q, first=False):
                pe.wait_ge(xn_done, NB + q + 1)
                if not first:
                    pe.wait_ge(m_lo, 2 * q - 1)
                for t in range(TT):
                    ins = T.transpose(bank[6][:, P * t:P * t + P], xn[:, t, :], EYE[:, :])
                ins.then_inc(a_xT, 1)
                pe.wait_ge(a_xT_sb, q + 1)
                MM(bank[7][:, :], WA[:, 0, :], xT[:, :], start=True, stop=True).then_inc(q_mm, 1)
                MM(bank[6][:, :], WA[:, 1, :], xT[:, :], start=True, stop=True).then_inc(k_mm, 1)
                pe.wait_ge(q_lo, q + 1)
                for t in range(TT):
                    ins = MM(bank[7][:, P * t:P * t + P], xT[:, P * t:P * t + P], WA[:, 2, :],
                             start=True, stop=True)
                ins.then_inc(v_mm, 1)

            def max_scores(b, par, bb, u):
                qt, hp = u // PAIRS, u % PAIRS
                wait(pe, max_done, UNITS * b + u - 1)
                for s in range(2):
                    ins = MM(bank[u % 2][:, SEQ * s:SEQ * s + SEQ],
                             QA[par][:, hp, SEQ * bb + P * qt:SEQ * bb + P * qt + P],
                             KA[par][:, 2 * hp + s, SEQ * bb:SEQ * bb + SEQ], start=True, stop=True)
                ins.then_inc(a_mm, 1)

            def scores(b, par, bb, u):
                hp, kt = u // 2, u % 2
                pe.wait_ge(exp_done, UNITS * b + u - 1 + CREDIT)
                for s in range(2):
                    ins = MM(bank[2 + u % 2][:, SEQ * s:SEQ * s + SEQ],
                             KA[par][:, 2 * hp + s, SEQ * bb + P * kt:SEQ * bb + P * kt + P],
                             QA[par][:, hp, SEQ * bb:SEQ * bb + SEQ], start=True, stop=True)
                ins.then_inc(b_mm, 1)

            def weigh(b, par, bb, g):
                pe.wait_ge(exp_done, UNITS * b + 4 * g + 4 + CREDIT)
                pe.wait_ge(o_out, 4 * b + g - 1 + CREDIT)
                for kt in range(2):
                    for h in range(4):
                        col = VW * (4 * g + h)
                        slot = (4 * g + 2 * (h // 2) + kt) % 8
                        ins = MM(bank[4 + g % 2][32 * h:32 * h + 32, 0:SEQ],
                                 V[par][:, 2 * bb + kt, col:col + 32],
                                 probs[:, slot, SEQ * (h % 2):SEQ * (h % 2) + SEQ],
                                 start=kt == 0, stop=kt == 1, tile_position=(0, 32 * h))
                ins.then_inc(pv_mm, 1)

            def max_rows(b):
                pe.wait_ge(max_done, UNITS * b + UNITS)
                for qt in range(2):
                    ins = T.transpose(bank[7][0:HEADS, P * qt:P * qt + P], neg_max[:, qt, :], EYE[:, :])
                ins.then_inc(m_T, 1)

            def tokens_of_o(b):
                pe.wait_ge(o_out, 4 * b + 4 + CREDIT)
                for qt in range(2):
                    for g in range(4):
                        ins = T.transpose(bank[6 + qt][:, P * g:P * g + P], oT[:, g, P * qt:P * qt + P],
                                          EYE[:, :])
                    ins.then_inc(o_tok, 1)

            def transpose_o(b):
                pe.wait_ge(o_norm, 2 * b + 2)
                for qt in range(2):
                    ins = T.transpose(bank[6][:, P * qt:P * qt + P], o_nat[:, qt, :], EYE[:, :])
                ins.then_inc(on_T, 1)

            def project_out(b):
                pe.wait_ge(on_T_sb, b + 1)
                for qt in range(2):
                    dst = bank[7][:, P * qt:P * qt + P]
                    MM(dst, onT[:, P * qt:P * qt + P], WA[:, 3, :], start=True, stop=False)
                    ins = MM(dst, ONES[0:1, :], BO[0:1, :], start=False, stop=True)
                ins.then_inc(y_mm, 1)

            def attend(b, pair, par, bb, more=True, before=True):
                npar, nbb = (par, 1) if bb == 0 else (1 - par, 0)
                if more and nbb == 0:
                    pe.wait_ge(qk_loaded, 256 * (pair + 2))
                    wait(pe, qa_cleared, 32 * pair)
                for u in range(UNITS + SKEW):
                    if u == 0 and before:
                        pe.wait_ge(m_lo, b + 1)
                        tokens_of_o(b - 1)
                    if u == 3 and before:
                        transpose_o(b - 1)
                    if u == 6 and before:
                        project_out(b - 1)
                    if more and u < UNITS:
                        max_scores(b + 1, npar, nbb, u)
                    if u == SKEW:
                        pe.wait_ge(m_loaded, 64 * (b + 1))
                    if u >= SKEW:
                        v = u - SKEW
                        scores(b, par, bb, v)
                        if v >= 5 and (v - 5) % 4 == 0:
                            weigh(b, par, bb, (v - 5) // 4)
                    if u == UNITS and more:
                        if before:
                            pe.wait_ge(att_added, b)
                        max_rows(b + 1)
                weigh(b, par, bb, 3)

            project_in(0, first=True)
            pe.wait_ge(pads_set, PADS)
            pe.wait_ge(qk_loaded, 256)
            for u in range(UNITS):
                max_scores(0, 0, 0, u)
            pe.wait_ge(v_set, 4 + 1)
            max_rows(0)

            def att_body(i, par, project=True, more=True, first=False):
                if project:
                    project_in(i + 1)
                    pe.wait_ge(v_set, 4 + i + 2)
                    pe.wait_ge(k_lo, i + 2)
                attend(2 * i, i, par, 0, before=not first)
                attend(2 * i + 1, i, par, 1, more=more)

            att_body(0, 0, first=True)
            att_body(1, 1)
            with pe.Fori(1, NPAIR // 2 - 1) as n:
                att_body(2 * n, 0)
                att_body(2 * n + 1, 1)
            att_body(NPAIR - 2, 0)
            att_body(NPAIR - 1, 1, project=False, more=False)
            pe.wait_ge(att_added, NBATCH - 1)
            tokens_of_o(NBATCH - 1)
            transpose_o(NBATCH - 1)
            project_out(NBATCH - 1)
            att_is_over(pe)
            ffn_phase(1, low_weights)


def kernel(**inputs):
    import numpy as np
    import concourse.bacc as bacc
    from concourse.bass_utils import run_bass_kernel_spmd

    g = {k.removeprefix("L0_"): np.asarray(v) for k, v in inputs.items()}
    x = g["attn_x"]

    def columns(v):
        return v.reshape(-1, P).T

    def k_major(w):
        return w.T.reshape(-1, P, w.shape[0]).transpose(1, 0, 2)

    ffn = [k_major(g[n]).reshape(P, -1, 512) for n in ("ffn_w1_w", "ffn_w2_w", "ffn_h1_w", "ffn_h2_w", "ffn_w3_w")]
    arrays = {
        "x": x.reshape(-1, P),
        "w_ffn": np.concatenate(ffn, axis=1),
        "w_att": np.stack([g["attn_" + n].T for n in ("Wq", "Wk", "Wv", "Wo")], axis=1),
        "s12": np.stack([columns(g["ffn_w1_s"]), columns(g["ffn_w2_s"])], axis=1),
        "sg": np.stack([columns(g["ffn_h1_s"]), columns(g["ffn_h2_s"])], axis=1),
        "s3": columns(g["ffn_w3_s"]),
        "bqk": np.stack([g["attn_bq"], g["attn_bk"]], axis=1),
        "bv": g["attn_bv"],
        "bo": g["attn_bo"].reshape(1, P),
        "eye": np.eye(P, dtype=np.float32),
    }
    arrays = {k: np.ascontiguousarray(v) for k, v in arrays.items()}
    nc = bacc.Bacc("TRN2", target_bir_lowering=False, num_devices=1)
    args = {k: nc.dram_tensor(k, v.shape, F32, kind="ExternalInput").ap() for k, v in arrays.items()}
    out = nc.dram_tensor("out", arrays["x"].shape, F32, kind="ExternalOutput").ap()
    macaron_kernel(nc, out=out, **args)
    r = run_bass_kernel_spmd(nc, [arrays], core_ids=[0])
    return r.results[0]["out"].reshape(x.shape)
```

```python
from contextlib import ExitStack

import concourse.bass as bass
from concourse import mybir

F32 = mybir.dt.float32
F32R = mybir.dt.float32r
I32 = mybir.dt.int32
ALU = mybir.AluOpType
ACT = mybir.ActivationFunctionType
AX = mybir.AxisListType

P = 128
BANKS = 8
TOK = 512
TT = TOK // P
HT = 4
SLOTS = 4
EPS = 1e-5
RSQRT_MAGIC = 0x5F3759DF
NEWTON = 3
HEADS, HD = 16, 8
PAIRS = HEADS // 2
SEQ = 256
SCALE = HD ** -0.5
VW = HD + 1
VROW = 168
UNITS = 16
SKEW = 4
CREDIT = 2
W_CHUNKS = 11
C_W1, C_W2, C_H1, C_H2, C_W3 = 0, 1, 2, 6, 10


def macaron_kernel(nc, x, w_ffn, w_att, s12, sg, s3, bqk, bv, bo, eye, out):
    NT = x.shape[0] // P
    NB = NT // TT
    NP = NB // 2
    NBATCH = x.shape[0] // SEQ
    NPAIR = NBATCH // 2
    x_t = x.rearrange("(t p) d -> p t d", p=P)
    out_t = out.rearrange("(t p) d -> p t d", p=P)
    qk_scratch = nc.dram_tensor("qk_scratch", (2, P, 4, 2 * SEQ), F32).ap()

    ctx = ExitStack()
    with ctx:
        def sb(name, shape, dt=F32, c=ctx):
            return c.enter_context(nc.sbuf_tensor(name, shape, dt))

        def sem(name):
            return ctx.enter_context(nc.semaphore(name))

        bank = [ctx.enter_context(nc.psum_tensor(f"bank{i}", [P, 512], F32)) for i in range(BANKS)]
        X = sb("X", [P, NT, P])
        WH = sb("WH", [P, W_CHUNKS, 512], F32R)
        WL = sb("WL", [P, W_CHUNKS, 512], F32R)
        WA = sb("WA", [P, 4, P])
        S12 = sb("S12", [P, 2, HT])
        SG = sb("SG", [P, 2, HT])
        S3 = sb("S3", [P, 1])
        S3H = sb("S3H", [P, 1])
        BQK = sb("BQK", [P, 2])
        BV = sb("BV", [P, TT, P])
        BO = sb("BO", [1, P])
        EYE = sb("EYE", [P, P])
        ONES = sb("ONES", [P, 2 * SEQ])
        stats = sb("stats", [P, 8, 6])
        moments = sb("moments", [P, 8, 2])
        var = sb("var", [P, 8])
        var_m = sb("var_m", [P, 8])
        C15 = sb("C15", [P, 8])
        scrap = sb("scrap", [P, 1])
        half = sb("half", [P, 8], I32)
        rstd = sb("rstd", [P, 8])
        newton = sb("newton", [P, 8])
        lo_max = sb("lo_max", [P, W_CHUNKS + 1])
        flag = sb("flag", [1, 1])
        xn = sb("xn", [P, 8, P])

        xT = sb("xT", [P, 2 * SEQ])

        ffn = ExitStack()
        x_hi = sb("x_hi", [P, 2, TOK], F32R, ffn)
        x_lo = sb("x_lo", [P, 2, TOK], F32R, ffn)
        raw = sb("raw", [P, 3, 512], F32, ffn)
        act_hi, act_lo = [None] * 3, [None] * 3
        act_hi[0] = sb("act0_hi", [P, 2, HT, TOK], F32R, ffn)
        act_lo[0] = sb("act0_lo", [P, 2, HT, TOK], F32R, ffn)
        silu = sb("silu", [P, SLOTS, TOK], F32, ffn)
        full = sb("full", [P, SLOTS, TOK], F32, ffn)
        for n in (1, 2):
            act_hi[n] = sb(f"act{n}_hi", [P, 2, HT, TOK], F32R, ffn)
            act_lo[n] = sb(f"act{n}_lo", [P, 2, HT, TOK], F32R, ffn)
        yT = sb("yT", [P, 2, TOK], F32, ffn)
        ffn.close()
        att = ExitStack()
        QA, KA = [None] * 2, [None] * 2
        qk = sb("qk", [P, 4, 2 * SEQ], F32R, att)
        V = [sb(f"V{i}", [P, TT, VROW], F32, att) for i in range(2)]
        for i in range(2):
            KA[i] = sb(f"KA{i}", [P, HEADS, 2 * SEQ], F32R, att)
            QA[i] = sb(f"QA{i}", [P, PAIRS, 2 * SEQ], F32R, att)
        probs = sb("probs", [P, 8, 2 * SEQ], F32, att)
        oT = sb("oT", [P, 4, SEQ], F32, att)
        o_sum = sb("o_sum", [P, 2, HEADS], F32, att)
        o_nat = sb("o_nat", [P, 2, P], F32, att)
        onT = sb("onT", [P, SEQ], F32, att)
        neg_max = sb("neg_max", [P, 2, HEADS], F32, att)
        m_parts = sb("m_parts", [HEADS, 2, SEQ], F32R, att)
        att.close()

        consts_in = sem("consts_in")
        x_in = sem("x_in")
        w_in = [sem(f"w_in{i}") for i in range(3)]
        ones_set = sem("ones_set")
        c15_set = sem("c15_set")
        s3_half = sem("s3_half")
        w_hi = sem("w_hi")
        w_lo = sem("w_lo")
        lo_reduced = sem("lo_reduced")
        flag_sum = sem("flag_sum")
        flag_set = sem("flag_set")
        stats_done = sem("stats_done")
        moments_done = sem("moments_done")
        var_done = sem("var_done")
        half_done = sem("half_done")
        guess_done = sem("guess_done")
        rstd_done = sem("rstd_done")
        newton_step = sem("newton_step")
        xn_done = sem("xn_done")
        xT_done = sem("xT_done")
        xhi_done = sem("xhi_done")
        xlo_done = sem("xlo_done")
        gate_mm = sem("gate_mm")
        up_mm = sem("up_mm")
        silu_done = sem("silu_done")
        h_full = sem("h_full")
        h_hi = sem("h_hi")
        h_lo = sem("h_lo")
        hid_mm = sem("hid_mm")
        g_hi = sem("g_hi")
        g_lo = sem("g_lo")
        out_mm = sem("out_mm")
        y_scaled = sem("y_scaled")
        y_back = sem("y_back")
        x_added = sem("x_added")
        stored = sem("stored")
        k_zero = sem("k_zero")
        pads_in = sem("pads_in")
        qa_cleared = sem("qa_cleared")
        a_xT = sem("a_xT")
        a_xT_sb = sem("a_xT_sb")
        q_mm = sem("q_mm")
        k_mm = sem("k_mm")
        v_mm = sem("v_mm")
        q_hi = sem("q_hi")
        q_lo = sem("q_lo")
        k_hi = sem("k_hi")
        k_lo = sem("k_lo")
        v_set = sem("v_set")
        qk_written = sem("qk_written")
        qk_loaded = sem("qk_loaded")
        a_mm = sem("a_mm")
        max_done = sem("max_done")
        m_T = sem("m_T")
        m_hi = sem("m_hi")
        m_lo = sem("m_lo")
        m_loaded = sem("m_loaded")
        b_mm = sem("b_mm")
        exp_done = sem("exp_done")
        pv_mm = sem("pv_mm")
        o_out = sem("o_out")
        o_tok = sem("o_tok")
        sums_inv = sem("sums_inv")
        o_norm = sem("o_norm")
        on_T = sem("on_T")
        on_T_sb = sem("on_T_sb")
        y_mm = sem("y_mm")
        att_added = sem("att_added")

        N_CONSTS = 11
        L2_LAST = HT * 2
        NORMS1 = NP + NPAIR - 1
        XN1 = NB + NPAIR
        L1_TILES = HT * 2
        HID_TILES = HT * 4

        block = ctx.enter_context(nc.Block())

        def wait(eng, s, v):
            if not isinstance(v, int) or v > 0:
                eng.wait_ge(s, v)

        def norm_of(q):
            return NP + q - 1

        def l2_over(eng):
            eng.wait_ge(hid_mm, NP * HID_TILES - L2_LAST)

        @block.sync
        def _(sp):
            def weights(c):
                if c >= 3:
                    sp.wait_ge(w_lo, c - 2)
                sp.dma_start(raw[:, c % 3, :], w_ffn[:, c, :]).then_inc(w_in[c % 3], 16)

            def load_x(i):
                sp.dma_start(X[:, 8 * i:8 * i + 8, :], x_t[:, 8 * i:8 * i + 8, :]).then_inc(x_in, 16)

            load_x(0)
            weights(0)
            weights(1)
            for dst, src in ((EYE[:, :], eye), (S12[:, :, :], s12), (SG[:, :, :], sg), (S3[:, :], s3),
                             (BQK[:, :], bqk), (BO[:, :], bo), (WA[:, :, :], w_att)):
                sp.dma_start(dst, src).then_inc(consts_in, 16)
            for t in range(TT):
                sp.dma_start(BV[:, t, :], bv.partition_broadcast(P)).then_inc(consts_in, 16)
            weights(2)
            for c in range(3, W_CHUNKS):
                weights(c)
                if c % 3 == 0:
                    load_x(c // 3)

            def pad(par):
                sp.wait_ge(k_zero, par + 1)
                for s in range(2):
                    row = 64 * s + 32
                    sp.dma_start(KA[par][row:row + 2, s:HEADS:2, :].bitcast(F32),
                                 ONES[0:2, :].unsqueeze(1).broadcast_to([2, PAIRS, 2 * SEQ])).then_inc(pads_in, 16)
                    sp.dma_start(QA[par][row:row + 32, :, :].bitcast(F32),
                                 KA[par][64:96, 0:HEADS:2, :].bitcast(F32)).then_inc(pads_in, 16)

            def write_qk(q, par):
                for c, lo in ((0, q_lo), (2, k_lo)):
                    sp.wait_ge(lo, q + 1)
                    sp.dma_start(qk_scratch[par][:, c:c + 2, :], qk[:, c:c + 2, :].bitcast(F32))\
                      .then_inc(qk_written, 16)

            def load_qk(q, par):
                sp.wait_ge(qk_written, 32 * q + 32)
                src = qk_scratch[par].rearrange("(hp s d) c t -> s c d hp t", s=2, d=HD)
                for s in range(2):
                    for r in range(4):
                        row = 64 * s + HD * r
                        sp.dma_start(QA[par][row:row + HD, :, :].bitcast(F32), src[s, r % 2])\
                          .then_inc(qk_loaded, 16)
                        sp.dma_start(KA[par][row:row + HD, s:HEADS:2, :].bitcast(F32), src[s, 2 + r // 2])\
                          .then_inc(qk_loaded, 16)

            def place_max(b, par, bb):
                sp.wait_ge(m_lo, b + 1)
                for s in range(2):
                    for c in range(2):
                        row = 64 * s + 32 + c
                        sp.dma_start(QA[par][row:row + 1, :, SEQ * bb:SEQ * bb + SEQ].bitcast(F32),
                                     m_parts[s:HEADS:2, c, :].bitcast(F32)).then_inc(m_loaded, 16)

            write_qk(0, 0)
            sp.wait_ge(g_lo, NP * HID_TILES + SLOTS)
            pad(0)
            load_qk(0, 0)
            write_qk(1, 1)
            sp.wait_ge(out_mm, NB)
            pad(1)
            load_qk(1, 1)
            place_max(0, 0, 0)

            def att_body(i, par, ahead=True, more=True):
                place_max(2 * i + 1, par, 1)
                if ahead:
                    write_qk(i + 2, par)
                if more:
                    place_max(2 * i + 2, 1 - par, 0)
                if ahead:
                    sp.wait_ge(b_mm, 2 * UNITS * (i + 1))
                    for s in range(2):
                        row = 64 * s + 32
                        sp.dma_start(QA[par][row:row + 2, :, :].bitcast(F32),
                                     KA[par][row + 2:row + 4, s:HEADS:2, :].bitcast(F32))\
                          .then_inc(qa_cleared, 16)
                    load_qk(i + 2, par)

            att_body(0, 0)
            att_body(1, 1)
            with sp.Fori(1, NPAIR // 2 - 1) as n:
                att_body(2 * n, 0)
                att_body(2 * n + 1, 1)
            att_body(NPAIR - 2, 0, ahead=False)
            att_body(NPAIR - 1, 1, ahead=False, more=False)

            with sp.Fori(0, NP) as i:
                sp.wait_ge(x_added, NB + 2 * i + 2 + CREDIT)
                sp.dma_start(out_t[:, bass.ds(8 * i, 8), :], X[:, bass.ds(8 * i, 8), :]).then_inc(stored, 16)
            sp.wait_ge(stored, 16 * NP)

        @block.gpsimd
        def _(pool):
            pool.memset(C15[:, :], 1.5).then_inc(c15_set, 1)
            pool.memset(ONES[:, :], 1.0).then_inc(ones_set, 1)
            pool.wait_ge(c15_set, 1)

            def rsqrt_steps(n, base, width=8):
                pool.wait_ge(guess_done, n + 1)
                v, y, a = var_m[:, 0:width], rstd[:, 0:width], newton[:, 0:width]
                k = 0
                for it in range(NEWTON):
                    last = it == NEWTON - 1
                    for step in range(4):
                        if step == 0:
                            ins = pool.tensor_tensor(a, y, y, op=ALU.mult)
                        elif step == 1:
                            ins = pool.tensor_tensor(a, a, v, op=ALU.mult)
                        elif step == 2:
                            ins = pool.tensor_tensor(a, a, C15[:, 0:width], op=ALU.add)
                        else:
                            ins = pool.tensor_tensor(y, y, a, op=ALU.mult)
                        if last and step == 3:
                            ins.then_inc(rstd_done, 1)
                        else:
                            k += 1
                            ins.then_inc(newton_step, 1)
                            pool.wait_ge(newton_step, base + k)

            K = 4 * NEWTON - 1

            def norms(first, last, width):
                with pool.Fori(first, last) as n:
                    rsqrt_steps(n, K * n, width)

            norms(0, NP + 1, 8)
            pool.wait_ge(rstd_done, NP + 1)
            l2_over(pool)
            pool.memset(KA[0][:, :, :].bitcast(F32), 0.0).then_inc(k_zero, 1)
            pool.wait_ge(k_zero, 1)
            pool.wait_ge(g_lo, NP * HID_TILES + SLOTS)
            pool.memset(KA[1][:, :, :].bitcast(F32), 0.0).then_inc(k_zero, 1)
            pool.wait_ge(k_zero, 2)
            norms(NP + 1, NORMS1, 4)
            norms(NORMS1, NORMS1 + NP, 8)

        @block.scalar
        def _(act):
            A = nc.scalar
            A.sem_inc(g_hi, CREDIT)
            A.sem_inc(exp_done, CREDIT)
            A.sem_inc(o_out, CREDIT)

            def weight_hi(c):
                act.wait_ge(w_in[c % 3], 16 * (c // 3 + 1))
                A.activation(WH[:, c, :], raw[:, c % 3, :], ACT.Copy).then_inc(w_hi, 1)

            def split_x(n, j):
                act.wait_ge(xT_done, n + 1)
                A.activation(x_hi[:, j, :], bank[6 + j][:, :], ACT.Copy).then_inc(xhi_done, 1)

            def layer1(n0, j, between={}):
                def hi(t):
                    act.wait_ge(h_full, n0 + t + 1)
                    A.activation(act_hi[0][:, j, t, :], silu[:, t, :], ACT.Copy).then_inc(h_hi, 1)
                for t in range(HT):
                    n = n0 + t
                    act.wait_ge(gate_mm, n + 1)
                    wait(act, h_lo, n - SLOTS + 1)
                    A.activation(silu[:, t, :], bank[t % 2][:, :], ACT.Silu,
                                 scale=S12[:, 0, t:t + 1]).then_inc(silu_done, 1)
                    if t >= 1:
                        hi(t - 1)
                    if t in between:
                        between[t]()
                hi(HT - 1)

            def hidden(n0, layer, j):
                for t in range(HT):
                    n = n0 + t
                    act.wait_ge(hid_mm, n + 1)
                    act.wait_ge(g_lo, n + 1)
                    A.activation(full[:, t, :], bank[4 + t % 2][:, :], ACT.Gelu,
                                 scale=SG[:, layer, t:t + 1])
                    A.activation(act_hi[1 + layer][:, j, t, :], bank[4 + t % 2][:, :], ACT.Gelu,
                                 scale=SG[:, layer, t:t + 1]).then_inc(g_hi, 1)

            def output(n, j):
                act.wait_ge(out_mm, n + 1)
                A.activation(yT[:, j, :], bank[6 + j][:, :], ACT.Copy, scale=S3H[:, 0:1]).then_inc(y_scaled, 1)

            def x_to_sbuf(q):
                act.wait_ge(a_xT, q + 1)
                A.activation(xT[:, :], bank[6][:, :], ACT.Copy).then_inc(a_xT_sb, 1)

            def high_q(q):
                act.wait_ge(q_mm, q + 1)
                wait(act, qk_written, 32 * q)
                A.activation(qk[:, 0, :], bank[7][:, :], ACT.Identity, bias=BQK[:, 0:1]).then_inc(q_hi, 1)

            def high_k(q):
                act.wait_ge(k_mm, q + 1)
                A.activation(qk[:, 2, :], bank[6][:, :], ACT.Identity, bias=BQK[:, 1:2]).then_inc(k_hi, 1)

            def ffn_phase(f):
                t1, t2, nb = f * NB * HT, f * NP * HID_TILES, f * NB

                def body(i, more=True):
                    g = t2 + HID_TILES * i
                    into_att = f == 0 and not more
                    hidden(g, 0, 0)
                    hidden(g + HT, 0, 1)
                    if into_att:
                        x_to_sbuf(0)
                    hidden(g + 2 * HT, 1, 0)
                    if into_att:
                        high_q(0)
                        high_k(0)
                    if more:
                        split_x(nb + 2 * i + 2, 0)
                        split_x(nb + 2 * i + 3, 1)
                    hidden(g + 3 * HT, 1, 1)
                    if more:
                        layer1(t1 + L1_TILES * (i + 1), 0, {1: lambda: output(nb + 2 * i, 0)})
                    else:
                        output(nb + 2 * i, 0)
                    output(nb + 2 * i + 1, 1)
                    if more:
                        layer1(t1 + L1_TILES * (i + 1) + HT, 1)

                if f == 0:
                    weight_hi(0)
                    weight_hi(1)
                    split_x(nb, 0)
                    for c in range(2, 5):
                        weight_hi(c)
                    split_x(nb + 1, 1)
                    layer1(t1, 0)
                    for c in range(5, W_CHUNKS):
                        weight_hi(c)
                    layer1(t1 + HT, 1)
                    act.wait_ge(s3_half, 1)
                else:
                    layer1(t1, 0, {2: lambda: o_to_sbuf(NBATCH - 1)})
                    layer1(t1 + HT, 1)
                with act.Fori(0, NP - 1) as i:
                    body(i)
                body(NP - 1, more=False)

            act.wait_ge(consts_in, 16 * N_CONSTS)
            ffn_phase(0)

            def exp_unit(b, u):
                n = UNITS * b + u
                act.wait_ge(b_mm, n + 1)
                act.wait_ge(pv_mm, 4 * b + u // 4 - 2 + 1 + CREDIT)
                A.activation(probs[:, u % 8, :], bank[2 + u % 2][:, :], ACT.Exp, scale=SCALE)\
                    .then_inc(exp_done, 1)

            def evacuate_o(b, g):
                act.wait_ge(pv_mm, 4 * b + g + 1 + CREDIT)
                A.activation(oT[:, g, :], bank[4 + g % 2][:, 0:SEQ], ACT.Copy).then_inc(o_out, 1)

            def split_max(b):
                act.wait_ge(m_T, b + 1)
                wait(act, m_loaded, 64 * b)
                A.activation(m_parts[:, 0, :], bank[7][0:HEADS, 0:SEQ], ACT.Copy).then_inc(m_hi, 1)

            def o_to_sbuf(b):
                act.wait_ge(on_T, b + 1)
                A.activation(onT[:, :], bank[6][:, 0:SEQ], ACT.Copy).then_inc(on_T_sb, 1)

            def attend(b, more=True, before=True, ahead=None, last=False):
                for u in range(UNITS + SKEW):
                    if u == 2 and before:
                        evacuate_o(b - 1, 3)
                    if u == 7 and before:
                        o_to_sbuf(b - 1)
                    if u >= SKEW:
                        v = u - SKEW
                        exp_unit(b, v)
                        if v >= 7 and (v - 7) % 4 == 0:
                            evacuate_o(b, (v - 7) // 4)
                    if ahead is not None and u == 11:
                        x_to_sbuf(ahead)
                    if ahead is not None and u == 13:
                        high_q(ahead)
                    if ahead is not None and u == 14:
                        high_k(ahead)
                    if last and u == 14:
                        act.wait_ge(qk_written, 32 * NPAIR)
                        split_x(NB, 0)
                        split_x(NB + 1, 1)
                    if u == 18 and more:
                        split_max(b + 1)

            x_to_sbuf(1)
            high_q(1)
            high_k(1)
            split_max(0)

            def att_body(i, ahead=True, more=True, first=False):
                attend(2 * i, before=not first)
                attend(2 * i + 1, more=more, ahead=i + 2 if ahead else None, last=not more)

            att_body(0, first=True)
            att_body(1)
            with act.Fori(1, NPAIR // 2 - 1) as n:
                att_body(2 * n)
                att_body(2 * n + 1)
            att_body(NPAIR - 2, ahead=False)
            att_body(NPAIR - 1, ahead=False, more=False)
            evacuate_o(NBATCH - 1, 3)
            ffn_phase(1)

        @block.vector
        def _(dve):
            D = nc.vector
            D.sem_inc(g_lo, SLOTS)
            D.sem_inc(x_added, CREDIT)

            def weight_lo(c):
                dve.wait_ge(w_hi, c + 1)
                D.tensor_tensor(WL[:, c, :], raw[:, c % 3, :], WH[:, c, :].bitcast(F32), op=ALU.subtract)\
                    .then_inc(w_lo, 1)

            def weight_lo_max(c):
                dve.wait_ge(w_lo, c + 1)
                D.tensor_reduce(lo_max[:, c:c + 1], WL[:, c, :].bitcast(F32), axis=AX.X, op=ALU.max,
                                apply_absolute_value=True).then_inc(lo_reduced, 1)

            def norm_steps(n, tile0, width=8):
                def s_stats():
                    for t in range(width):
                        ins = D.bn_stats(stats[:, t, :], X[:, bass.ds(tile0 + t, 1), :])
                    ins.then_inc(stats_done, 1)

                def s_moments():
                    dve.wait_ge(stats_done, n + 1)
                    D.memset(scrap[:, 0:1], 0.0)
                    for t in range(width):
                        ins = D.bn_aggr(moments[:, t, :], stats[:, t, :])
                    ins.then_inc(moments_done, 1)

                def s_var():
                    dve.wait_ge(moments_done, n + 1)
                    D.tensor_scalar(var_m[:, 0:width], moments[:, 0:width, 1], EPS, -0.5, ALU.add, ALU.mult)
                    D.tensor_scalar(var[:, 0:width], moments[:, 0:width, 1], EPS, None, ALU.add)\
                        .then_inc(var_done, 1)

                def s_half():
                    dve.wait_ge(var_done, n + 1)
                    D.tensor_scalar(half[:, 0:width], var[:, 0:width].bitcast(I32), 1, None,
                                    ALU.arith_shift_right).then_inc(half_done, 1)

                def s_guess():
                    dve.wait_ge(half_done, n + 1)
                    D.tensor_scalar(rstd[:, 0:width].bitcast(I32), half[:, 0:width], -1.0,
                                    float(RSQRT_MAGIC), ALU.mult, ALU.add).then_inc(guess_done, 1)

                return [s_stats, s_moments, s_var, s_half, s_guess]

            def normalise(n, tile0, t0, width=4):
                dve.wait_ge(rstd_done, n + 1)
                for t in range(t0, t0 + width):
                    ins = D.tensor_scalar(xn[:, t:t + 1, :], X[:, bass.ds(tile0 + t - t0, 1), :],
                                          moments[:, t, 0:1], rstd[:, t:t + 1], ALU.subtract, ALU.mult)
                ins.then_inc(xn_done, 1)

            def low_x(n, j):
                dve.wait_ge(xhi_done, n + 1)
                D.tensor_tensor(x_lo[:, j, :], bank[6 + j][:, :], x_hi[:, j, :].bitcast(F32), op=ALU.subtract)\
                    .then_inc(xlo_done, 1)

            def layer1(n0, j, between={}):
                def lo(t):
                    dve.wait_ge(h_hi, n0 + t + 1)
                    D.tensor_tensor(act_lo[0][:, j, t, :], silu[:, t, :], act_hi[0][:, j, t, :].bitcast(F32),
                                    op=ALU.subtract).then_inc(h_lo, 1)
                for t in range(HT):
                    n = n0 + t
                    dve.wait_ge(silu_done, n + 1)
                    dve.wait_ge(up_mm, n + 1)
                    D.scalar_tensor_tensor(out=silu[:, t, :], in0=bank[2 + t % 2][:, :],
                                           scalar=S12[:, 1, t:t + 1], in1=silu[:, t, :],
                                           op0=ALU.mult, op1=ALU.mult).then_inc(h_full, 1)
                    if t >= 1:
                        lo(t - 1)
                    if t in between:
                        between[t]()
                lo(HT - 1)

            def hidden(n0, layer, j, between=()):
                for t in range(HT):
                    dve.wait_ge(g_hi, n0 + t + 1 + CREDIT)
                    D.tensor_tensor(act_lo[1 + layer][:, j, t, :], full[:, t, :],
                                    act_hi[1 + layer][:, j, t, :].bitcast(F32), op=ALU.subtract)\
                        .then_inc(g_lo, 1)
                    for step in between[t:t + 1]:
                        step()

            def residual(n, tile0, j):
                dve.wait_ge(y_back, n + 1)
                xs = X[:, bass.ds(tile0, TT), :]
                D.tensor_tensor(xs, bank[6 + j][:, :].rearrange("p (t d) -> p t d", t=TT), xs, op=ALU.add)\
                    .then_inc(x_added, 1)

            def low_qk(q, c):
                hi, lo, b = ((q_hi, q_lo, 7), (k_hi, k_lo, 6))[c // 2]
                dve.wait_ge(hi, q + 1)
                D.scalar_tensor_tensor(out=qk[:, c + 1, :], in0=bank[b][:, :],
                                       scalar=BQK[:, c // 2:c // 2 + 1], in1=qk[:, c, :].bitcast(F32),
                                       op0=ALU.add, op1=ALU.subtract).then_inc(lo, 1)

            def set_v(q, par):
                dve.wait_ge(v_mm, q + 1)
                for t in range(TT):
                    ins = D.tensor_tensor(
                        V[par][:, t, 0:HEADS * VW].rearrange("p (h v) -> p h v", v=VW)[:, :, 0:HD],
                        bank[7][:, P * t:P * t + P].rearrange("p (h v) -> p h v", v=HD),
                        BV[:, t, :].rearrange("p (h v) -> p h v", v=HD), op=ALU.add)
                ins.then_inc(v_set, 1)

            def clear_v():
                for par in range(2):
                    D.memset(V[par][:, :, :], 0.0).then_inc(v_set, 1)
                dve.wait_ge(v_set, 2)
                for par in range(2):
                    ones_of = V[par][:, :, 0:HEADS * VW].rearrange("p t (h v) -> p t h v", v=VW)
                    D.memset(ones_of[:, :, :, HD:VW], 1.0).then_inc(v_set, 1)

            def max_unit(b, u):
                dve.wait_ge(a_mm, UNITS * b + u + 1)
                qt, hp = u // PAIRS, u % PAIRS
                D.tensor_reduce(neg_max[:, qt, 2 * hp:2 * hp + 2],
                                bank[u % 2][:, :].rearrange("p (h k) -> p h k", h=2), axis=AX.X,
                                op=ALU.max, negate=True).then_inc(max_done, 1)

            def low_max(b):
                dve.wait_ge(m_hi, b + 1)
                D.tensor_tensor(m_parts[:, 1, :], bank[7][0:HEADS, 0:SEQ], m_parts[:, 0, :].bitcast(F32),
                                op=ALU.subtract).then_inc(m_lo, 1)

            def o_of(qt):
                return bank[6 + qt][:, :].rearrange("p (h v) -> p h v", v=32)

            def norm_o(b):
                for qt in range(2):
                    dve.wait_ge(o_tok, 2 * b + qt + 1)
                    D.reciprocal(o_sum[:, qt, :], o_of(qt)[:, :, HD]).then_inc(sums_inv, 1)

            def scale_o(b):
                for qt in range(2):
                    dve.wait_ge(sums_inv, 2 * b + qt + 1)
                    D.tensor_tensor(o_nat[:, qt, :].rearrange("p (h v) -> p h v", v=HD),
                                    o_of(qt)[:, :, 0:HD],
                                    o_sum[:, qt, :].unsqueeze(2).broadcast_to([P, HEADS, HD]),
                                    op=ALU.mult).then_inc(o_norm, 1)

            def add_att(b, tile0):
                dve.wait_ge(y_mm, b + 1)
                xs = X[:, bass.ds(tile0, 2), :]
                D.tensor_tensor(xs, bank[7][:, 0:SEQ].rearrange("p (t d) -> p t d", t=2), xs, op=ALU.add)\
                    .then_inc(att_added, 1)

            def ffn_phase(f):
                t1, t2, nb, n0 = f * NB * HT, f * NP * HID_TILES, f * NB, f * NORMS1

                def body(i, more=True):
                    g = t2 + HID_TILES * i
                    into_att = f == 0 and not more
                    norm = more or into_att
                    n, tile0 = n0 + i + 1, 8 * i + 8
                    if into_att:
                        tile0 = 0
                        clear_v()
                    if norm:
                        if f == 0 and more:
                            dve.wait_ge(x_in, 16 * i + 32)
                        steps = norm_steps(n, tile0)
                        steps[0]()
                        hidden(g, 0, 0, steps[1:])
                    else:
                        hidden(g, 0, 0)
                    hidden(g + HT, 0, 1)
                    if norm:
                        normalise(n, tile0, 0)
                        normalise(n, tile0 + 4, 4)
                    hidden(g + 2 * HT, 1, 0)
                    if more:
                        low_x(nb + 2 * i + 2, 0)
                        low_x(nb + 2 * i + 3, 1)
                    if into_att:
                        low_qk(0, 0)
                        low_qk(0, 2)
                    hidden(g + 3 * HT, 1, 1)
                    if into_att:
                        set_v(0, 0)
                    if more:
                        layer1(t1 + L1_TILES * (i + 1), 0)
                        layer1(t1 + L1_TILES * (i + 1) + HT, 1)
                    residual(nb + 2 * i, 8 * i, 0)
                    residual(nb + 2 * i + 1, 8 * i + 4, 1)

                if f == 0:
                    dve.wait_ge(x_in, 16)
                    for step in norm_steps(n0, 0):
                        step()
                    weight_lo(0)
                    weight_lo(1)
                    normalise(n0, 0, 0)
                    normalise(n0, 4, 4)
                    low_x(nb, 0)
                    for c in range(2, 5):
                        weight_lo(c)
                    low_x(nb + 1, 1)
                    dve.wait_ge(consts_in, 16 * N_CONSTS)
                    D.tensor_scalar(S3H[:, :], S3[:, :], 0.5, None, ALU.mult).then_inc(s3_half, 1)
                    layer1(t1, 0)
                    for c in range(5, W_CHUNKS):
                        weight_lo(c)
                        weight_lo_max(c - 1)
                    for c in (0, 1, 2, 3, W_CHUNKS - 1):
                        weight_lo_max(c)
                    dve.wait_ge(lo_reduced, W_CHUNKS)
                    D.tensor_reduce(lo_max[:, W_CHUNKS:W_CHUNKS + 1], lo_max[:, 0:W_CHUNKS], axis=AX.X,
                                    op=ALU.max).then_inc(lo_reduced, 1)
                    layer1(t1 + HT, 1)
                    dve.wait_ge(flag_sum, 1)
                    D.tensor_copy(flag[:, :], bank[4][0:1, 0:1]).then_inc(flag_set, 1)
                else:
                    b = NBATCH - 1
                    layer1(t1, 0, {0: lambda: norm_o(b), 1: lambda: scale_o(b)})
                    layer1(t1 + HT, 1, {0: lambda: add_att(b, 2 * b)})
                with dve.Fori(0, NP - 1) as i:
                    body(i)
                body(NP - 1, more=False)

            ffn_phase(0)

            def attend(b, more=True, before=True, steps=(), norm=None, ahead=None, v_pair=None):
                for u in range(UNITS + SKEW):
                    if more and u < UNITS:
                        max_unit(b + 1, u)
                    if u == 2 and norm is not None:
                        n, tile0, width = norm
                        normalise(n, tile0, 0)
                        if width > 4:
                            normalise(n, tile0 + 4, 4)
                    if u == 4 and before:
                        norm_o(b - 1)
                    if u == 5 and before:
                        scale_o(b - 1)
                    if u == 11 and before:
                        add_att(b - 1, 2 * b - 2)
                    if u >= 9:
                        for step in steps[u - 9:u - 8]:
                            step()
                    if u == 14 and ahead is not None:
                        low_qk(ahead, 0)
                    if u == 15 and ahead is not None:
                        low_qk(ahead, 2)
                    if u == 14 and v_pair is not None:
                        set_v(*v_pair)
                    if u == 18 and more:
                        low_max(b + 1)
                if not more:
                    low_x(NB, 0)
                    low_x(NB + 1, 1)

            for u in range(UNITS):
                max_unit(0, u)
                if u == 5:
                    low_qk(1, 0)
                if u == 6:
                    low_qk(1, 2)
            low_max(0)

            def att_body(i, par, ahead=True, more=True, first=False):
                if ahead:
                    q = i + 2
                    steps, norm = norm_steps(norm_of(q), 4 * q, 4), (norm_of(q), 4 * q, 4)
                elif not more:
                    steps, norm = norm_steps(NORMS1, 0), (NORMS1, 0, 8)
                else:
                    steps, norm = (), None
                attend(2 * i, before=not first, steps=steps, v_pair=(i + 1, 1 - par) if more else None)
                attend(2 * i + 1, more=more, norm=norm, ahead=i + 2 if ahead else None)

            att_body(0, 0, first=True)
            att_body(1, 1)
            with dve.Fori(1, NPAIR // 2 - 1) as n:
                att_body(2 * n, 0)
                att_body(2 * n + 1, 1)
            att_body(NPAIR - 2, 0, ahead=False)
            att_body(NPAIR - 1, 1, ahead=False, more=False)
            ffn_phase(1)

        @block.tensor
        def _(pe):
            T = nc.tensor
            T.sem_inc(pv_mm, CREDIT)
            MM = T.matmul

            def split_mm(dst, w, xs, general):
                todo = [(wh, part) for (wh, _), (xh, xl) in zip(w, xs) for part in (xh, xl)]
                if general:
                    todo += [(wl, part) for (_, wl), (xh, xl) in zip(w, xs) for part in (xh, xl)]
                for k, (a, b) in enumerate(todo):
                    ins = MM(dst, a, b, start=k == 0, stop=k == len(todo) - 1)
                return ins

            def w_of(c, t):
                return WH[:, c, P * t:P * t + P], WL[:, c, P * t:P * t + P]

            def layer1(n0, nblk, j, general, between={}):
                pe.wait_ge(xlo_done, nblk + 1)
                xs = [(x_hi[:, j, :], x_lo[:, j, :])]
                for t in range(HT):
                    n = n0 + t
                    wait(pe, silu_done, n - 1)
                    split_mm(bank[t % 2][:, :], [w_of(C_W1, t)], xs, general).then_inc(gate_mm, 1)
                    wait(pe, h_full, n - 1)
                    split_mm(bank[2 + t % 2][:, :], [w_of(C_W2, t)], xs, general).then_inc(up_mm, 1)
                    if t in between:
                        between[t]()

            def inputs_of(layer, j):
                return [(act_hi[layer][:, j, k, :], act_lo[layer][:, j, k, :]) for k in range(HT)]

            def hidden(n0, layer, j, ready_sem, ready, general):
                pe.wait_ge(ready_sem, ready)
                xs = inputs_of(layer, j)
                c0 = (C_H1, C_H2)[layer]
                for t in range(HT):
                    pe.wait_ge(g_hi, n0 + t + 1)
                    split_mm(bank[4 + t % 2][:, :], [w_of(c0 + k, t) for k in range(HT)], xs, general)\
                        .then_inc(hid_mm, 1)

            def output(nblk, j, g_ready, general):
                pe.wait_ge(g_lo, g_ready + SLOTS)
                split_mm(bank[6 + j][:, :], [w_of(C_W3, k) for k in range(HT)], inputs_of(2, j), general)\
                    .then_inc(out_mm, 1)

            def transpose_x(nx, j):
                pe.wait_ge(xn_done, nx + 1)
                for t in range(TT):
                    ins = T.transpose(bank[6 + j][:, P * t:P * t + P], xn[:, 4 * j + t, :], EYE[:, :])
                ins.then_inc(xT_done, 1)

            def transpose_y(nblk, j):
                pe.wait_ge(y_scaled, nblk + 1)
                for t in range(TT):
                    ins = T.transpose(bank[6 + j][:, P * t:P * t + P], yT[:, j, P * t:P * t + P], EYE[:, :])
                ins.then_inc(y_back, 1)

            def transpose_att(q, t0):
                pe.wait_ge(xn_done, NB + q + 1)
                for t in range(TT):
                    ins = T.transpose(bank[6][:, P * t:P * t + P], xn[:, t0 + t, :], EYE[:, :])
                ins.then_inc(a_xT, 1)

            def project_q(q):
                pe.wait_ge(a_xT_sb, q + 1)
                MM(bank[7][:, :], WA[:, 0, :], xT[:, :], start=True, stop=True).then_inc(q_mm, 1)

            def project_k(q):
                pe.wait_ge(a_xT_sb, q + 1)
                MM(bank[6][:, :], WA[:, 1, :], xT[:, :], start=True, stop=True).then_inc(k_mm, 1)

            def project_v(q):
                for t in range(TT):
                    ins = MM(bank[7][:, P * t:P * t + P], xT[:, P * t:P * t + P], WA[:, 2, :],
                             start=True, stop=True)
                ins.then_inc(v_mm, 1)

            def max_scores(b, par, bb, u):
                qt, hp = u // PAIRS, u % PAIRS
                wait(pe, max_done, UNITS * b + u - 1)
                for s in range(2):
                    ins = MM(bank[u % 2][:, SEQ * s:SEQ * s + SEQ],
                             QA[par][:, hp, SEQ * bb + P * qt:SEQ * bb + P * qt + P],
                             KA[par][:, 2 * hp + s, SEQ * bb:SEQ * bb + SEQ], start=True, stop=True)
                ins.then_inc(a_mm, 1)

            def scores(b, par, bb, u):
                hp, kt = u // 2, u % 2
                pe.wait_ge(exp_done, UNITS * b + u - 1 + CREDIT)
                for s in range(2):
                    ins = MM(bank[2 + u % 2][:, SEQ * s:SEQ * s + SEQ],
                             KA[par][:, 2 * hp + s, SEQ * bb + P * kt:SEQ * bb + P * kt + P],
                             QA[par][:, hp, SEQ * bb:SEQ * bb + SEQ], start=True, stop=True)
                ins.then_inc(b_mm, 1)

            def weigh(b, par, bb, g):
                pe.wait_ge(exp_done, UNITS * b + 4 * g + 4 + CREDIT)
                pe.wait_ge(o_out, 4 * b + g - 1 + CREDIT)
                for kt in range(2):
                    for h in range(4):
                        col = VW * (4 * g + h)
                        slot = (4 * g + 2 * (h // 2) + kt) % 8
                        ins = MM(bank[4 + g % 2][32 * h:32 * h + 32, 0:SEQ],
                                 V[par][:, 2 * bb + kt, col:col + 32],
                                 probs[:, slot, SEQ * (h % 2):SEQ * (h % 2) + SEQ],
                                 start=kt == 0, stop=kt == 1, tile_position=(0, 32 * h))
                ins.then_inc(pv_mm, 1)

            def max_rows(b):
                pe.wait_ge(max_done, UNITS * b + UNITS)
                for qt in range(2):
                    ins = T.transpose(bank[7][0:HEADS, P * qt:P * qt + P], neg_max[:, qt, :], EYE[:, :])
                ins.then_inc(m_T, 1)

            def tokens_of_o(b):
                pe.wait_ge(o_out, 4 * b + 4 + CREDIT)
                for qt in range(2):
                    for g in range(4):
                        ins = T.transpose(bank[6 + qt][:, P * g:P * g + P], oT[:, g, P * qt:P * qt + P],
                                          EYE[:, :])
                    ins.then_inc(o_tok, 1)

            def transpose_o(b):
                pe.wait_ge(o_norm, 2 * b + 2)
                for qt in range(2):
                    ins = T.transpose(bank[6][:, P * qt:P * qt + P], o_nat[:, qt, :], EYE[:, :])
                ins.then_inc(on_T, 1)

            def project_out(b):
                pe.wait_ge(on_T_sb, b + 1)
                for qt in range(2):
                    dst = bank[7][:, P * qt:P * qt + P]
                    MM(dst, onT[:, P * qt:P * qt + P], WA[:, 3, :], start=True, stop=False)
                    ins = MM(dst, ONES[0:1, 0:P], BO[0:1, :], start=False, stop=True)
                ins.then_inc(y_mm, 1)

            def ffn_bodies(f, general):
                t1, t2, nb, nx = f * NB * HT, f * NP * HID_TILES, f * NB, f * XN1

                def body(i, more=True):
                    g = t2 + HID_TILES * i
                    hl = t1 + L1_TILES * i
                    into_att = f == 0 and not more
                    hidden(g, 0, 0, h_lo, hl + HT, general)
                    hidden(g + HT, 0, 1, h_lo, hl + 2 * HT, general)
                    if into_att:
                        pe.wait_ge(x_added, nb + 2 * i + CREDIT)
                        transpose_att(0, 0)
                    hidden(g + 2 * HT, 1, 0, g_lo, g + HT + SLOTS, general)
                    if more:
                        for j in range(2):
                            pe.wait_ge(x_added, nb + 2 * i - 1 + j + CREDIT)
                            transpose_x(nx + 2 * i + 2 + j, j)
                    if into_att:
                        project_q(0)
                        project_k(0)
                    hidden(g + 3 * HT, 1, 1, g_lo, g + 2 * HT + SLOTS, general)
                    if more:
                        def output_b():
                            pe.wait_ge(xlo_done, nb + 2 * i + 4)
                            output(nb + 2 * i + 1, 1, g + 4 * HT, general)
                        layer1(hl + L1_TILES, nb + 2 * i + 2, 0, general,
                               {1: lambda: output(nb + 2 * i, 0, g + 3 * HT, general), 3: output_b})
                        layer1(hl + L1_TILES + HT, nb + 2 * i + 3, 1, general)
                    else:
                        if into_att:
                            pe.wait_ge(q_lo, 1)
                            project_v(0)
                            pe.wait_ge(k_lo, 1)
                        else:
                            pe.wait_ge(x_added, nb + 2 * i + CREDIT)
                        output(nb + 2 * i, 0, g + 3 * HT, general)
                        if into_att:
                            pe.wait_ge(v_set, 4 + 1)
                        output(nb + 2 * i + 1, 1, g + 4 * HT, general)
                    transpose_y(nb + 2 * i, 0)
                    transpose_y(nb + 2 * i + 1, 1)

                if f == 1:
                    b = NBATCH - 1
                    weigh(b, 1, 1, 3)

                    def tokens():
                        pe.wait_ge(xlo_done, NB + 2)
                        tokens_of_o(b)
                    layer1(t1, nb, 0, general,
                           {1: tokens, 2: lambda: transpose_o(b), 3: lambda: project_out(b)})
                    layer1(t1 + HT, nb + 1, 1, general)
                    pe.wait_ge(att_added, NBATCH)
                with pe.Fori(0, NP - 1) as i:
                    body(i)
                body(NP - 1, more=False)

            def ffn_phase(f, low_weights):
                if f == 0:
                    pe.wait_ge(consts_in, 16 * N_CONSTS)
                    transpose_x(0, 0)
                    transpose_x(1, 1)
                    pe.wait_ge(w_lo, 2)
                    layer1(0, 0, 0, True)
                    layer1(HT, 1, 1, True)
                    pe.wait_ge(ones_set, 1)
                    pe.wait_ge(lo_reduced, W_CHUNKS + 1)
                    MM(bank[4][0:1, 0:1], ONES[:, 0:1], lo_max[:, W_CHUNKS:W_CHUNKS + 1],
                       start=True, stop=True).then_inc(flag_sum, 1)
                    pe.wait_ge(flag_set, 1)
                    pe.reg_load(low_weights, flag[0:1, 0:1].bitcast(I32))
                with pe.If_ne(low_weights, 0):
                    ffn_bodies(f, True)
                with pe.Else():
                    ffn_bodies(f, False)

            low_weights = T.alloc_register("low_weights")
            ffn_phase(0, low_weights)

            def attend(b, pair, par, bb, more=True, before=True, ahead=None, v_pair=None):
                npar, nbb = (par, 1) if bb == 0 else (1 - par, 0)
                if more and nbb == 0:
                    pe.wait_ge(pads_in, 64 * (npar + 1))
                    pe.wait_ge(qk_loaded, 256 * (pair + 2))
                    if not (isinstance(pair, int) and pair == 0):
                        pe.wait_ge(qa_cleared, 32 * pair)
                for u in range(UNITS + SKEW):
                    if more and u < UNITS:
                        max_scores(b + 1, npar, nbb, u)
                    if u == 1 and before:
                        weigh(b - 1, *((1 - par, 1) if bb == 0 else (par, 0)), 3)
                    if u == 3 and before:
                        pe.wait_ge(m_lo, b + 1)
                        tokens_of_o(b - 1)
                    if u == 6 and before:
                        transpose_o(b - 1)
                    if u == 9 and before:
                        project_out(b - 1)
                    if u == 10 and ahead is not None:
                        transpose_att(ahead, 0)
                    if u == 12 and ahead is not None:
                        pe.wait_ge(att_added, b)
                        project_q(ahead)
                    if u == 13 and ahead is not None:
                        project_k(ahead)
                    if u == 13 and v_pair is not None:
                        if before:
                            pe.wait_ge(att_added, b)
                        project_v(v_pair)
                    if u == 12 and not more:
                        pe.wait_ge(att_added, b)
                        transpose_x(XN1, 0)
                        transpose_x(XN1 + 1, 1)
                    if u == SKEW:
                        pe.wait_ge(m_loaded, 64 * (b + 1))
                    if u >= SKEW:
                        v = u - SKEW
                        scores(b, par, bb, v)
                        if v >= 5 and (v - 5) % 4 == 0:
                            weigh(b, par, bb, (v - 5) // 4)
                    if u == UNITS + 1 and more:
                        if v_pair is not None:
                            pe.wait_ge(v_set, 4 + v_pair + 1)
                        elif ahead is not None:
                            pe.wait_ge(q_lo, ahead + 1)
                        else:
                            pe.wait_ge(att_added, b)
                        max_rows(b + 1)

            pe.wait_ge(x_added, NB + CREDIT)
            transpose_att(1, 4)
            pe.wait_ge(pads_in, 64)
            pe.wait_ge(qk_loaded, 256)
            for u in range(UNITS):
                max_scores(0, 0, 0, u)
                if u == 2:
                    project_q(1)
                if u == 3:
                    project_k(1)
            pe.wait_ge(q_lo, 2)
            max_rows(0)

            def att_body(i, par, ahead=True, more=True, first=False):
                attend(2 * i, i, par, 0, before=not first, v_pair=i + 1 if more else None)
                attend(2 * i + 1, i, par, 1, more=more, ahead=i + 2 if ahead else None)

            att_body(0, 0, first=True)
            att_body(1, 1)
            with pe.Fori(1, NPAIR // 2 - 1) as n:
                att_body(2 * n, 0)
                att_body(2 * n + 1, 1)
            att_body(NPAIR - 2, 0, ahead=False)
            att_body(NPAIR - 1, 1, ahead=False, more=False)
            ffn_phase(1, low_weights)


def kernel(**inputs):
    import numpy as np
    import concourse.bacc as bacc
    from concourse.bass_utils import run_bass_kernel_spmd

    g = {k.removeprefix("L0_"): np.asarray(v) for k, v in inputs.items()}
    x = g["attn_x"]

    def columns(v):
        return v.reshape(-1, P).T

    def k_major(w):
        return w.T.reshape(-1, P, w.shape[0]).transpose(1, 0, 2)

    ffn = [k_major(g[n]).reshape(P, -1, 512) for n in ("ffn_w1_w", "ffn_w2_w", "ffn_h1_w", "ffn_h2_w", "ffn_w3_w")]
    arrays = {
        "x": x.reshape(-1, P),
        "w_ffn": np.concatenate(ffn, axis=1),
        "w_att": np.stack([g["attn_" + n].T for n in ("Wq", "Wk", "Wv", "Wo")], axis=1),
        "s12": np.stack([columns(g["ffn_w1_s"]), columns(g["ffn_w2_s"])], axis=1),
        "sg": np.stack([columns(g["ffn_h1_s"]), columns(g["ffn_h2_s"])], axis=1),
        "s3": columns(g["ffn_w3_s"]),
        "bqk": np.stack([g["attn_bq"], g["attn_bk"]], axis=1),
        "bv": g["attn_bv"],
        "bo": g["attn_bo"].reshape(1, P),
        "eye": np.eye(P, dtype=np.float32),
    }
    arrays = {k: np.ascontiguousarray(v) for k, v in arrays.items()}
    nc = bacc.Bacc("TRN2", target_bir_lowering=False, num_devices=1)
    args = {k: nc.dram_tensor(k, v.shape, F32, kind="ExternalInput").ap() for k, v in arrays.items()}
    out = nc.dram_tensor("out", arrays["x"].shape, F32, kind="ExternalOutput").ap()
    macaron_kernel(nc, out=out, **args)
    r = run_bass_kernel_spmd(nc, [arrays], core_ids=[0])
    return r.results[0]["out"].reshape(x.shape)
```

```python
from contextlib import ExitStack

import concourse.bass as bass
from concourse import mybir

F32 = mybir.dt.float32
F32R = mybir.dt.float32r
I32 = mybir.dt.int32
ALU = mybir.AluOpType
ACT = mybir.ActivationFunctionType
AX = mybir.AxisListType

P = 128
BANKS = 8
TOK = 512
TT = TOK // P
HT = 4
SLOTS = 4
EPS = 1e-5
RSQRT_MAGIC = 0x5F3759DF
NEWTON = 3
HEADS, HD = 16, 8
PAIRS = HEADS // 2
SEQ = 256
SCALE = HD ** -0.5
VW = HD + 1
VROW = 168
UNITS = 16
GROUPS = 4
SKEW = 8
GATE_BANKS = (0, 1, 4, 0, 1, 4, 0, 1)
UP_BANKS = (2, 3, 5, 2, 3, 5, 2, 3)
A_BANKS = (0, 1, 5) * 4 + (0, 1, 5, 1)
CREDIT = 2
W_CHUNKS = 11
C_W1, C_W2, C_H1, C_H2, C_W3 = 0, 1, 2, 6, 10
W_GROUPS = ((0, 1), (1, 2), (2, 3), (3, 5), (5, 7), (7, 9), (9, 11))
W_RAW = 3


def macaron_kernel(nc, x, w_ffn, w_att, s12, sg, s3, bqk, bv, bo, eye, out):
    NT = x.shape[0] // P
    NB = NT // TT
    NP = NB // 2
    NBATCH = x.shape[0] // SEQ
    NPAIR = NBATCH // 2
    x_t = x.rearrange("(t p) d -> p t d", p=P)
    out_t = out.rearrange("(t p) d -> p t d", p=P)
    qk_scratch = nc.dram_tensor("qk_scratch", (2, 2, 2, 2, 2, HD, PAIRS, SEQ), F32).ap()

    ctx = ExitStack()
    with ctx:
        def sb(name, shape, dt=F32, c=ctx):
            return c.enter_context(nc.sbuf_tensor(name, shape, dt))

        def sem(name):
            return ctx.enter_context(nc.semaphore(name))

        bank = [ctx.enter_context(nc.psum_tensor(f"bank{i}", [P, 512], F32)) for i in range(BANKS)]
        X = sb("X", [P, NT, P])
        WH = sb("WH", [P, W_CHUNKS, 512], F32R)
        WL = sb("WL", [P, W_CHUNKS, 512], F32R)
        WA = sb("WA", [P, 4, P])
        S12 = sb("S12", [P, 2, HT])
        SG = sb("SG", [P, 2, HT])
        S3 = sb("S3", [P, 1])
        S3H = sb("S3H", [P, 1])
        BQK = sb("BQK", [P, 2])
        BV = sb("BV", [P, TT, P])
        BO = sb("BO", [P, P])
        EYE = sb("EYE", [P, P])
        ONES = sb("ONES", [P, 2 * SEQ])
        stats = sb("stats", [P, 8, 6])
        moments = sb("moments", [P, 8, 2])
        var = sb("var", [P, 8])
        var_m = sb("var_m", [P, 8])
        C15 = sb("C15", [P, 8])
        scrap = sb("scrap", [P, 1])
        half = sb("half", [P, 8], I32)
        rstd = sb("rstd", [P, 8])
        newton = sb("newton", [P, 8])
        lo_max = sb("lo_max", [P, len(W_GROUPS) + 1])
        flag = sb("flag", [1, 1])
        xn = sb("xn", [P, 8, P])
        xT = sb("xT", [P, 2 * SEQ])
        neg_max = sb("neg_max", [P, 2, 2, HEADS])

        ffn = ExitStack()
        x_hi = sb("x_hi", [P, 2, TOK], F32R, ffn)
        x_lo = sb("x_lo", [P, 2, TOK], F32R, ffn)
        raw = sb("raw", [P, W_RAW, 512], F32, ffn)
        act_hi, act_lo = [None] * 3, [None] * 3
        act_hi[0] = sb("act0_hi", [P, 2, HT, TOK], F32R, ffn)
        act_lo[0] = sb("act0_lo", [P, 2, HT, TOK], F32R, ffn)
        silu = sb("silu", [P, SLOTS, TOK], F32, ffn)
        full = sb("full", [P, SLOTS, TOK], F32, ffn)
        start = ExitStack()
        raw_rest = sb("raw_rest", [P, W_CHUNKS - W_RAW, 512], F32, start)
        start.close()
        for n in (1, 2):
            act_hi[n] = sb(f"act{n}_hi", [P, 2, HT, TOK], F32R, ffn)
            act_lo[n] = sb(f"act{n}_lo", [P, 2, HT, TOK], F32R, ffn)
        yT = sb("yT", [P, 2, TOK], F32, ffn)
        ffn.close()
        att = ExitStack()
        QA, KA = [None] * 2, [None] * 2
        qk = sb("qk", [P, 4, 2 * SEQ], F32R, att)
        V = [sb(f"V{i}", [P, TT, VROW], F32, att) for i in range(2)]
        for i in range(2):
            KA[i] = sb(f"KA{i}", [P, 2, 2, PAIRS, SEQ], F32R, att)
            QA[i] = sb(f"QA{i}", [P, 2, PAIRS, SEQ], F32R, att)
        probs = sb("probs", [P, 8, 2 * SEQ], F32, att)
        oT = sb("oT", [P, 4, SEQ], F32, att)
        o_sum = sb("o_sum", [P, 2, HEADS], F32, att)
        o_nat = sb("o_nat", [P, 2, P], F32, att)
        onT = sb("onT", [P, SEQ], F32, att)
        m_parts = sb("m_parts", [HEADS, 2, SEQ], F32R, att)
        att.close()

        consts_in = sem("consts_in")
        x_in = sem("x_in")
        x_rest_in = sem("x_rest_in")
        eye_in = sem("eye_in")
        att_in = sem("att_in")
        w_in = [sem(f"w_in{k}") for k in range(len(W_GROUPS))]
        ones_set = sem("ones_set")
        c15_set = sem("c15_set")
        s3_half = sem("s3_half")
        w_hi = sem("w_hi")
        w_lo = sem("w_lo")
        w_lo_rest = sem("w_lo_rest")
        lo_reduced = sem("lo_reduced")
        flag_sum = sem("flag_sum")
        flag_set = sem("flag_set")
        stats_done = sem("stats_done")
        moments_done = sem("moments_done")
        var_done = sem("var_done")
        half_done = sem("half_done")
        guess_done = sem("guess_done")
        rstd_done = sem("rstd_done")
        newton_step = sem("newton_step")
        xn_done = sem("xn_done")
        xT_done = sem("xT_done")
        xhi_done = sem("xhi_done")
        xlo_done = sem("xlo_done")
        gate_mm = sem("gate_mm")
        up_mm = sem("up_mm")
        silu_done = sem("silu_done")
        h_full = sem("h_full")
        h_hi = sem("h_hi")
        h_lo = sem("h_lo")
        hid_mm = sem("hid_mm")
        g_hi = sem("g_hi")
        g_lo = sem("g_lo")
        out_mm = sem("out_mm")
        y_scaled = sem("y_scaled")
        y_back = sem("y_back")
        x_added = sem("x_added")
        stored = sem("stored")
        pads_in = [[sem(f"pads_in{p}{bb}") for bb in range(2)] for p in range(2)]
        k_zero = sem("k_zero")
        qa_cleared = sem("qa_cleared")
        a_xT = sem("a_xT")
        a_xT_sb = sem("a_xT_sb")
        q_mm = sem("q_mm")
        k_mm = sem("k_mm")
        v_mm = sem("v_mm")
        q_hi = sem("q_hi")
        q_lo = sem("q_lo")
        k_hi = sem("k_hi")
        k_lo = sem("k_lo")
        v_set = sem("v_set")
        qk_written = [sem(f"qk_written{bb}") for bb in range(2)]
        qk_loaded = [[sem(f"qk_loaded{p}{bb}") for bb in range(2)] for p in range(2)]
        a_mm = sem("a_mm")
        max_done = sem("max_done")
        m_T = sem("m_T")
        m_hi = sem("m_hi")
        m_lo = sem("m_lo")
        m_loaded = sem("m_loaded")
        b_mm = sem("b_mm")
        exp_done = sem("exp_done")
        pv_mm = sem("pv_mm")
        o_out = sem("o_out")
        o_tok = sem("o_tok")
        sums_inv = sem("sums_inv")
        o_norm = sem("o_norm")
        on_T = sem("on_T")
        on_T_sb = sem("on_T_sb")
        y_mm = sem("y_mm")
        att_added = sem("att_added")
        bias_added = sem("bias_added")

        N_CONSTS = 3
        N_ATT_CONSTS = 3 + TT
        L2_LAST = HT * 2
        NORMS1 = NP + NPAIR - 1
        XN1 = NB + NPAIR
        L1_TILES = HT * 2
        HID_TILES = HT * 4

        block = ctx.enter_context(nc.Block())

        def wait(eng, s, v):
            if not isinstance(v, int) or v > 0:
                eng.wait_ge(s, v)

        def raw_of(k):
            a, b = W_GROUPS[k]
            return raw[:, a:b, :] if b <= W_RAW else raw_rest[:, a - W_RAW:b - W_RAW, :]

        def part_of(w, k):
            a, b = W_GROUPS[k]
            return w[:, a:b, :]

        def a_unit(u):
            return u // 8, u // 2 % GROUPS, u % 2

        def b_unit(v):
            return v // 4, v // 2 % 2, v % 2

        def in_step(u, prev, own=True):
            at = [(0, u - SKEW)] if own else []
            if prev:
                at.append((1, u - SKEW + UNITS))
            return [(d, v) for d, v in at if 0 <= v < UNITS + 3]

        def norm_of(q):
            return NP + q - 1

        def l2_over(eng):
            eng.wait_ge(hid_mm, NP * HID_TILES - L2_LAST)

        @block.sync
        def _(sp):
            def weights(k):
                a, b = W_GROUPS[k]
                sp.dma_start(raw_of(k), w_ffn[:, a:b, :]).then_inc(w_in[k], 16)

            def load_x(i, arrived):
                sp.dma_start(X[:, 8 * i:8 * i + 8, :], x_t[:, 8 * i:8 * i + 8, :]).then_inc(arrived, 16)

            load_x(0, x_in)
            weights(0)
            weights(1)
            sp.dma_start(EYE[:, :], eye).then_inc(eye_in, 16)
            weights(2)
            for dst, src in ((S12[:, :, :], s12), (SG[:, :, :], sg), (S3[:, :], s3)):
                sp.dma_start(dst, src).then_inc(consts_in, 16)
            for k in range(3, len(W_GROUPS)):
                weights(k)
            load_x(1, x_rest_in)
            for dst, src in ((BQK[:, :], bqk), (BO[:, :], bo.partition_broadcast(P)), (WA[:, :, :], w_att)):
                sp.dma_start(dst, src).then_inc(att_in, 16)
            for t in range(TT):
                sp.dma_start(BV[:, t, :], bv.partition_broadcast(P)).then_inc(att_in, 16)
            for i in range(2, NP):
                load_x(i, x_rest_in)

            def pad(par, bb):
                sp.wait_ge(k_zero, par + 1)
                for s in range(2):
                    row = 64 * s + 32
                    sp.dma_start(KA[par][row:row + 2, s, bb, :, :].bitcast(F32)
                                 .rearrange("r (c hp) t -> r c (hp t)", hp=2),
                                 ONES[0:2, :].unsqueeze(1).broadcast_to([2, PAIRS // 2, 2 * SEQ]))\
                      .then_inc(pads_in[par][bb], 16)
                    sp.dma_start(QA[par][row:row + 32, bb, :, :].bitcast(F32),
                                 KA[par][64:96, 0, bb, :, :].bitcast(F32)).then_inc(pads_in[par][bb], 16)

            def clear_max(par):
                for s in range(2):
                    row = 64 * s + 32
                    sp.dma_start(QA[par][row:row + 2, :, :, :].bitcast(F32),
                                 KA[par][row + 2:row + 4, s, :, :, :].bitcast(F32)).then_inc(qa_cleared, 16)

            def write_qk(q, par, bb):
                for w, lo in ((0, q_lo), (1, k_lo)):
                    sp.wait_ge(lo, q + 1)
                    for s in range(2):
                        sp.dma_start(qk_scratch[par, w, bb, s].rearrange("c d hp t -> (d hp) c t"),
                                     qk[64 * s:64 * s + 64, 2 * w:2 * w + 2, SEQ * bb:SEQ * bb + SEQ]
                                     .bitcast(F32)).then_inc(qk_written[bb], 16)

            def load_k(q, par, bb):
                sp.wait_ge(qk_written[bb], 64 * q + 64)
                for s in range(2):
                    for c in range(2):
                        row = 64 * s + 16 * c
                        sp.dma_start(KA[par][row:row + 16, s, bb, :, :].bitcast(F32)
                                     .rearrange("r hp t -> r (hp t)"),
                                     qk_scratch[par, 1, bb, s, c].rearrange("d hp t -> d (hp t)").unsqueeze(0)
                                     .broadcast_to([2, HD, PAIRS * SEQ])).then_inc(qk_loaded[par][bb], 16)

            def load_q(par, bb):
                for s in range(2):
                    sp.dma_start(QA[par][64 * s:64 * s + 32, bb, :, :].bitcast(F32)
                                 .rearrange("r hp t -> r (hp t)"),
                                 qk_scratch[par, 0, bb, s].rearrange("c d hp t -> (c d) (hp t)").unsqueeze(0)
                                 .broadcast_to([2, 2 * HD, PAIRS * SEQ])).then_inc(qk_loaded[par][bb], 16)

            def place_max(b, par, bb):
                for c, part in enumerate((m_hi, m_lo)):
                    sp.wait_ge(part, b + 1)
                    for s in range(2):
                        row = 64 * s + 32 + c
                        sp.dma_start(QA[par][row:row + 1, bb, :, :].bitcast(F32),
                                     m_parts[s:HEADS:2, c, :].bitcast(F32)).then_inc(m_loaded, 16)

            pad(0, 0)
            write_qk(0, 0, 0)
            load_k(0, 0, 0)
            load_q(0, 0)
            write_qk(0, 0, 1)
            sp.wait_ge(g_lo, NP * HID_TILES + SLOTS)
            pad(0, 1)
            load_k(0, 0, 1)
            load_q(0, 1)
            sp.wait_ge(out_mm, NB)
            pad(1, 0)
            pad(1, 1)
            write_qk(1, 1, 0)

            def att_body(i, par, first=False, ahead=True, load=True):
                place_max(2 * i, par, 0)
                if load:
                    if not first:
                        sp.wait_ge(b_mm, 2 * UNITS * i)
                        clear_max(1 - par)
                    for bb in range(2):
                        if first and bb == 1:
                            write_qk(1, 1, 1)
                        load_k(i + 1, 1 - par, bb)
                        load_q(1 - par, bb)
                place_max(2 * i + 1, par, 1)
                if ahead:
                    write_qk(i + 2, par, 0)
                    write_qk(i + 2, par, 1)

            att_body(0, 0, first=True)
            att_body(1, 1)
            with sp.Fori(1, NPAIR // 2 - 1) as n:
                att_body(2 * n, 0)
                att_body(2 * n + 1, 1)
            att_body(NPAIR - 2, 0, ahead=False)
            att_body(NPAIR - 1, 1, ahead=False, load=False)

            with sp.Fori(0, NP) as i:
                sp.wait_ge(x_added, NB + 2 * i + 2 + CREDIT)
                sp.dma_start(out_t[:, bass.ds(8 * i, 8), :], X[:, bass.ds(8 * i, 8), :]).then_inc(stored, 16)
            sp.wait_ge(stored, 16 * NP)

        @block.gpsimd
        def _(pool):
            pool.memset(C15[:, :], 1.5).then_inc(c15_set, 1)
            pool.memset(ONES[:, :], 1.0).then_inc(ones_set, 1)
            pool.wait_ge(c15_set, 1)

            def rsqrt_steps(n, base, width=8):
                pool.wait_ge(guess_done, n + 1)
                v, y, a = var_m[:, 0:width], rstd[:, 0:width], newton[:, 0:width]
                k = 0
                for it in range(NEWTON):
                    last = it == NEWTON - 1
                    for step in range(4):
                        if step == 0:
                            ins = pool.tensor_tensor(a, y, y, op=ALU.mult)
                        elif step == 1:
                            ins = pool.tensor_tensor(a, a, v, op=ALU.mult)
                        elif step == 2:
                            ins = pool.tensor_tensor(a, a, C15[:, 0:width], op=ALU.add)
                        else:
                            ins = pool.tensor_tensor(y, y, a, op=ALU.mult)
                        if last and step == 3:
                            ins.then_inc(rstd_done, 1)
                        else:
                            k += 1
                            ins.then_inc(newton_step, 1)
                            pool.wait_ge(newton_step, base + k)

            K = 4 * NEWTON - 1

            def norms(first, last, width):
                with pool.Fori(first, last) as n:
                    rsqrt_steps(n, K * n, width)

            rsqrt_steps(0, 0)
            for k in range(2, len(W_GROUPS)):
                pool.wait_ge(w_hi, k + 1)
                pool.tensor_tensor(part_of(WL, k), raw_of(k), part_of(WH, k).bitcast(F32), op=ALU.subtract)\
                    .then_inc(w_lo_rest, 1)
            norms(1, NP + 1, 8)
            pool.wait_ge(rstd_done, NP + 1)
            l2_over(pool)
            pool.memset(KA[0][:, :, :, :, :].bitcast(F32), 0.0).then_inc(k_zero, 1)
            pool.wait_ge(k_zero, 1)
            pool.wait_ge(g_lo, NP * HID_TILES + SLOTS)
            pool.memset(KA[1][:, :, :, :, :].bitcast(F32), 0.0).then_inc(k_zero, 1)
            pool.wait_ge(k_zero, 2)

            def add_bias(b):
                pool.wait_ge(att_added, b + 1)
                xs = X[:, bass.ds(2 * b, 2), :]
                pool.tensor_tensor(xs, xs, BO[:, :].unsqueeze(1).broadcast_to([P, 2, P]), op=ALU.add)\
                    .then_inc(bias_added, 1)

            def norm_for(i):
                n = norm_of(i + 2)
                rsqrt_steps(n, K * n, 4)

            pool.wait_ge(att_in, 16 * N_ATT_CONSTS)
            norm_for(0)
            with pool.Fori(1, NPAIR - 2) as i:
                add_bias(2 * i - 2)
                norm_for(i)
                add_bias(2 * i - 1)
            with pool.Fori(2 * NPAIR - 6, NBATCH - 3) as b:
                add_bias(b)
            rsqrt_steps(NORMS1, K * NORMS1)
            with pool.Fori(NBATCH - 3, NBATCH) as b:
                add_bias(b)
            norms(NORMS1 + 1, NORMS1 + NP, 8)

        @block.scalar
        def _(act):
            A = nc.scalar
            A.sem_inc(g_hi, CREDIT)
            A.sem_inc(exp_done, CREDIT)

            def weight_hi(k):
                act.wait_ge(w_in[k], 16)
                A.activation(part_of(WH, k), raw_of(k), ACT.Copy).then_inc(w_hi, 1)

            def split_x(n, j):
                act.wait_ge(xT_done, n + 1)
                A.activation(x_hi[:, j, :], bank[6 + j][:, :], ACT.Copy).then_inc(xhi_done, 1)

            def product_hi(n0, t):
                act.wait_ge(h_full, n0 + t + 1)
                A.activation(act_hi[0][:, t // HT, t % HT, :], silu[:, t % SLOTS, :], ACT.Copy).then_inc(h_hi, 1)

            def layer1(n0, between={}):
                for t in range(L1_TILES):
                    act.wait_ge(gate_mm, n0 + t + 1)
                    wait(act, h_lo, n0 + t - SLOTS + 1)
                    A.activation(silu[:, t % SLOTS, :], bank[GATE_BANKS[t]][:, :], ACT.Silu,
                                 scale=S12[:, 0, t % HT:t % HT + 1]).then_inc(silu_done, 1)
                    if t >= 1:
                        product_hi(n0, t - 1)
                    if t in between:
                        between[t]()

            def hidden(n0, layer, j, between={}):
                for t in range(HT):
                    n = n0 + t
                    act.wait_ge(hid_mm, n + 1)
                    act.wait_ge(g_lo, n + 1)
                    A.activation(full[:, t, :], bank[4 + t % 2][:, :], ACT.Gelu,
                                 scale=SG[:, layer, t:t + 1])
                    A.activation(act_hi[1 + layer][:, j, t, :], bank[4 + t % 2][:, :], ACT.Gelu,
                                 scale=SG[:, layer, t:t + 1]).then_inc(g_hi, 1)
                    if t in between:
                        between[t]()

            def output(n, j):
                act.wait_ge(out_mm, n + 1)
                A.activation(yT[:, j, :], bank[6 + j][:, :], ACT.Copy, scale=S3H[:, 0:1]).then_inc(y_scaled, 1)

            def x_to_sbuf(q):
                act.wait_ge(a_xT, q + 1)
                A.activation(xT[:, :], bank[6][:, :], ACT.Copy).then_inc(a_xT_sb, 1)

            def high_q(q):
                act.wait_ge(q_mm, q + 1)
                for bb in range(2):
                    wait(act, qk_written[bb], 64 * q)
                A.activation(qk[:, 0, :], bank[7][:, :], ACT.Identity, bias=BQK[:, 0:1]).then_inc(q_hi, 1)

            def high_k(q):
                act.wait_ge(k_mm, q + 1)
                A.activation(qk[:, 2, :], bank[6][:, :], ACT.Identity, bias=BQK[:, 1:2]).then_inc(k_hi, 1)

            def ffn_phase(f):
                t1, t2, nb = f * NB * HT, f * NP * HID_TILES, f * NB

                def body(i, first=False, more=True):
                    g = t2 + HID_TILES * i
                    into_att = f == 0 and not more
                    before = nb + 2 * i - 2
                    side = {0: lambda: product_hi(t1 + L1_TILES * i, L1_TILES - 1)}
                    if not first:
                        side |= {1: lambda: output(before, 0), 2: lambda: output(before + 1, 1)}
                    hidden(g, 0, 0, side)
                    hidden(g + HT, 0, 1)
                    hidden(g + 2 * HT, 1, 0, {1: lambda: x_to_sbuf(0)} if into_att else {})
                    if into_att:
                        high_q(0)
                        high_k(0)
                    if more:
                        split_x(nb + 2 * i + 2, 0)
                        split_x(nb + 2 * i + 3, 1)
                    hidden(g + 3 * HT, 1, 1)
                    if more:
                        layer1(t1 + L1_TILES * (i + 1))
                    else:
                        output(nb + 2 * i, 0)
                        output(nb + 2 * i + 1, 1)

                if f == 0:
                    weight_hi(0)
                    weight_hi(1)
                    split_x(nb, 0)
                    weight_hi(2)
                    split_x(nb + 1, 1)
                    weight_hi(3)
                    act.wait_ge(consts_in, 16 * N_CONSTS)
                    layer1(t1, {t: lambda k=t + 4: weight_hi(k) for t in range(3)})
                    act.wait_ge(s3_half, 1)
                else:
                    layer1(t1, {3: lambda: o_to_sbuf(NBATCH - 1)})
                body(0, first=True)
                with act.Fori(1, NP - 1) as i:
                    body(i)
                body(NP - 1, more=False)

            ffn_phase(0)

            def exp_unit(b, v):
                act.wait_ge(b_mm, UNITS * b + v + 1)
                act.wait_ge(pv_mm, GROUPS * b + v // 4 - 2 + 1 + CREDIT)
                A.activation(probs[:, v % 8, :], bank[2 + v % 2][:, :], ACT.Exp, scale=SCALE)\
                    .then_inc(exp_done, 1)

            def evacuate_o(b, half):
                act.wait_ge(pv_mm, GROUPS * b + 2 * half + 2 + CREDIT)
                A.activation(oT[:, 2 * half:2 * half + 2, :], bank[4][:, :], ACT.Copy).then_inc(o_out, 1)

            def split_max(b):
                act.wait_ge(m_T, b + 1)
                wait(act, m_loaded, 64 * b)
                A.activation(m_parts[:, 0, :], bank[6][0:HEADS, 0:SEQ], ACT.Copy).then_inc(m_hi, 1)

            def o_to_sbuf(b):
                act.wait_ge(on_T, b + 1)
                A.activation(onT[:, :], bank[6][:, 0:SEQ], ACT.Copy).then_inc(on_T_sb, 1)

            def attend(b, prev=True, own=True, steps=UNITS, ahead=None):
                for u in range(steps):
                    for d, v in in_step(u, prev, own):
                        if v < UNITS:
                            exp_unit(b - d, v)
                        if v == 10:
                            evacuate_o(b - d, 0)
                        if v == UNITS + 2:
                            evacuate_o(b - d, 1)
                    if u == 1 and own:
                        split_max(b)
                    if u == 5 and ahead is not None:
                        x_to_sbuf(ahead)
                    if u == 7 and ahead is not None:
                        high_q(ahead)
                    if u == 8 and ahead is not None:
                        high_k(ahead)
                    if u == 15 and own and prev:
                        o_to_sbuf(b - 1)
                    if u == 5 and not own:
                        for bb in range(2):
                            act.wait_ge(qk_written[bb], 64 * NPAIR)
                        split_x(NB, 0)
                        split_x(NB + 1, 1)

            x_to_sbuf(1)
            high_q(1)
            high_k(1)

            def att_body(i, ahead=True, first=False):
                attend(2 * i, prev=not first)
                attend(2 * i + 1, ahead=i + 2 if ahead else None)

            att_body(0, first=True)
            att_body(1)
            with act.Fori(1, NPAIR // 2 - 1) as n:
                att_body(2 * n)
                att_body(2 * n + 1)
            att_body(NPAIR - 2, ahead=False)
            att_body(NPAIR - 1, ahead=False)
            attend(NBATCH, own=False, steps=SKEW + 3)
            ffn_phase(1)

        @block.vector
        def _(dve):
            D = nc.vector
            D.sem_inc(g_lo, SLOTS)
            D.sem_inc(x_added, CREDIT)

            def weight_lo(k):
                dve.wait_ge(w_hi, k + 1)
                D.tensor_tensor(part_of(WL, k), raw_of(k), part_of(WH, k).bitcast(F32), op=ALU.subtract)\
                    .then_inc(w_lo, 1)

            def weight_lo_max(k):
                if k < 2:
                    dve.wait_ge(w_lo, k + 1)
                else:
                    dve.wait_ge(w_lo_rest, k - 1)
                D.tensor_reduce(lo_max[:, k:k + 1], part_of(WL, k).bitcast(F32), axis=AX.XY, op=ALU.max,
                                apply_absolute_value=True).then_inc(lo_reduced, 1)

            def all_lo_max():
                G = len(W_GROUPS)
                dve.wait_ge(lo_reduced, G)
                D.tensor_reduce(lo_max[:, G:G + 1], lo_max[:, 0:G], axis=AX.X, op=ALU.max)\
                    .then_inc(lo_reduced, 1)

            def take_flag():
                dve.wait_ge(flag_sum, 1)
                D.tensor_copy(flag[:, :], bank[6][0:1, 0:1]).then_inc(flag_set, 1)

            def norm_steps(n, tile0, width=8, biased=0):
                def s_stats():
                    if biased:
                        dve.wait_ge(bias_added, biased)
                    for t in range(width):
                        ins = D.bn_stats(stats[:, t, :], X[:, bass.ds(tile0 + t, 1), :])
                    ins.then_inc(stats_done, 1)

                def s_moments():
                    dve.wait_ge(stats_done, n + 1)
                    D.memset(scrap[:, 0:1], 0.0)
                    for t in range(width):
                        ins = D.bn_aggr(moments[:, t, :], stats[:, t, :])
                    ins.then_inc(moments_done, 1)

                def s_var():
                    dve.wait_ge(moments_done, n + 1)
                    D.tensor_scalar(var_m[:, 0:width], moments[:, 0:width, 1], EPS, -0.5, ALU.add, ALU.mult)
                    D.tensor_scalar(var[:, 0:width], moments[:, 0:width, 1], EPS, None, ALU.add)\
                        .then_inc(var_done, 1)

                def s_half():
                    dve.wait_ge(var_done, n + 1)
                    D.tensor_scalar(half[:, 0:width], var[:, 0:width].bitcast(I32), 1, None,
                                    ALU.arith_shift_right).then_inc(half_done, 1)

                def s_guess():
                    dve.wait_ge(half_done, n + 1)
                    D.tensor_scalar(rstd[:, 0:width].bitcast(I32), half[:, 0:width], -1.0,
                                    float(RSQRT_MAGIC), ALU.mult, ALU.add).then_inc(guess_done, 1)

                return [s_stats, s_moments, s_var, s_half, s_guess]

            def normalise(n, tile0, t0, width=4):
                dve.wait_ge(rstd_done, n + 1)
                for t in range(t0, t0 + width):
                    ins = D.tensor_scalar(xn[:, t:t + 1, :], X[:, bass.ds(tile0 + t - t0, 1), :],
                                          moments[:, t, 0:1], rstd[:, t:t + 1], ALU.subtract, ALU.mult)
                ins.then_inc(xn_done, 1)

            def low_x(n, j):
                dve.wait_ge(xhi_done, n + 1)
                D.tensor_tensor(x_lo[:, j, :], bank[6 + j][:, :], x_hi[:, j, :].bitcast(F32), op=ALU.subtract)\
                    .then_inc(xlo_done, 1)

            def product_lo(n0, t):
                dve.wait_ge(h_hi, n0 + t + 1)
                D.tensor_tensor(act_lo[0][:, t // HT, t % HT, :], silu[:, t % SLOTS, :],
                                act_hi[0][:, t // HT, t % HT, :].bitcast(F32), op=ALU.subtract)\
                    .then_inc(h_lo, 1)

            def layer1(n0, between={}):
                for t in range(L1_TILES):
                    dve.wait_ge(silu_done, n0 + t + 1)
                    dve.wait_ge(up_mm, n0 + t + 1)
                    D.scalar_tensor_tensor(out=silu[:, t % SLOTS, :], in0=bank[UP_BANKS[t]][:, :],
                                           scalar=S12[:, 1, t % HT:t % HT + 1], in1=silu[:, t % SLOTS, :],
                                           op0=ALU.mult, op1=ALU.mult).then_inc(h_full, 1)
                    if t >= 1:
                        product_lo(n0, t - 1)
                    if t in between:
                        between[t]()

            def hidden(n0, layer, j, between=()):
                for t in range(HT):
                    dve.wait_ge(g_hi, n0 + t + 1 + CREDIT)
                    D.tensor_tensor(act_lo[1 + layer][:, j, t, :], full[:, t, :],
                                    act_hi[1 + layer][:, j, t, :].bitcast(F32), op=ALU.subtract)\
                        .then_inc(g_lo, 1)
                    for step in between[t:t + 1]:
                        step()

            def residual(n, tile0, j):
                dve.wait_ge(y_back, n + 1)
                xs = X[:, bass.ds(tile0, TT), :]
                D.tensor_tensor(xs, bank[6 + j][:, :].rearrange("p (t d) -> p t d", t=TT), xs, op=ALU.add)\
                    .then_inc(x_added, 1)

            def low_qk(q, c):
                hi, lo, b = ((q_hi, q_lo, 7), (k_hi, k_lo, 6))[c // 2]
                dve.wait_ge(hi, q + 1)
                D.scalar_tensor_tensor(out=qk[:, c + 1, :], in0=bank[b][:, :],
                                       scalar=BQK[:, c // 2:c // 2 + 1], in1=qk[:, c, :].bitcast(F32),
                                       op0=ALU.add, op1=ALU.subtract).then_inc(lo, 1)

            def set_v(q, par):
                dve.wait_ge(v_mm, q + 1)
                for t in range(TT):
                    ins = D.tensor_tensor(
                        V[par][:, t, 0:HEADS * VW].rearrange("p (h v) -> p h v", v=VW)[:, :, 0:HD],
                        bank[7][:, P * t:P * t + P].rearrange("p (h v) -> p h v", v=HD),
                        BV[:, t, :].rearrange("p (h v) -> p h v", v=HD), op=ALU.add)
                ins.then_inc(v_set, 1)

            def clear_v():
                for par in range(2):
                    D.memset(V[par][:, :, :], 0.0).then_inc(v_set, 1)
                dve.wait_ge(v_set, 2)
                for par in range(2):
                    ones_of = V[par][:, :, 0:HEADS * VW].rearrange("p t (h v) -> p t h v", v=VW)
                    D.memset(ones_of[:, :, :, HD:VW], 1.0).then_inc(v_set, 1)

            def max_unit(b, bb, u):
                dve.wait_ge(a_mm, UNITS * b + u + 1)
                qt, j, s = a_unit(u)
                D.tensor_reduce(neg_max[:, bb, qt, 4 * j + s:4 * j + 4:2],
                                bank[A_BANKS[u]][:, :].rearrange("p (h k) -> p h k", h=2), axis=AX.X,
                                op=ALU.max, negate=True).then_inc(max_done, 1)

            def low_max(b):
                dve.wait_ge(m_hi, b + 1)
                D.tensor_tensor(m_parts[:, 1, :], bank[6][0:HEADS, 0:SEQ], m_parts[:, 0, :].bitcast(F32),
                                op=ALU.subtract).then_inc(m_lo, 1)

            def o_of(qt):
                return bank[6 + qt][:, :].rearrange("p (h v) -> p h v", v=32)

            def norm_o(b):
                for qt in range(2):
                    dve.wait_ge(o_tok, 2 * b + qt + 1)
                    D.reciprocal(o_sum[:, qt, :], o_of(qt)[:, :, HD]).then_inc(sums_inv, 1)

            def scale_o(b):
                for qt in range(2):
                    dve.wait_ge(sums_inv, 2 * b + qt + 1)
                    D.tensor_tensor(o_nat[:, qt, :].rearrange("p (h v) -> p h v", v=HD),
                                    o_of(qt)[:, :, 0:HD],
                                    o_sum[:, qt, :].unsqueeze(2).broadcast_to([P, HEADS, HD]),
                                    op=ALU.mult).then_inc(o_norm, 1)

            def add_att(b, tile0):
                dve.wait_ge(y_mm, b + 1)
                xs = X[:, bass.ds(tile0, 2), :]
                D.tensor_tensor(xs, bank[7][:, 0:SEQ].rearrange("p (t d) -> p t d", t=2), xs, op=ALU.add)\
                    .then_inc(att_added, 1)

            def ffn_phase(f):
                t1, t2, nb, n0 = f * NB * HT, f * NP * HID_TILES, f * NB, f * NORMS1

                def body(i, first=False, more=True):
                    g = t2 + HID_TILES * i
                    into_att = f == 0 and not more
                    norm = more or into_att
                    n, tile0 = n0 + i + 1, 8 * i + 8
                    if into_att:
                        tile0 = 0
                        clear_v()
                    steps = norm_steps(n, tile0) if norm else []
                    for step in steps[0:1]:
                        step()

                    def first_step():
                        product_lo(t1 + L1_TILES * i, L1_TILES - 1)
                        for step in steps[1:2]:
                            step()
                    hidden(g, 0, 0, [first_step] + steps[2:])
                    hidden(g + HT, 0, 1)
                    if not first:
                        residual(nb + 2 * i - 2, 8 * i - 8, 0)
                        residual(nb + 2 * i - 1, 8 * i - 4, 1)
                    if norm:
                        normalise(n, tile0, 0)
                        normalise(n, tile0 + 4, 4)
                    hidden(g + 2 * HT, 1, 0)
                    if more:
                        low_x(nb + 2 * i + 2, 0)
                        low_x(nb + 2 * i + 3, 1)
                    if into_att:
                        low_qk(0, 0)
                        low_qk(0, 2)
                    hidden(g + 3 * HT, 1, 1)
                    if into_att:
                        set_v(0, 0)
                        for u in range(3):
                            max_unit(0, 0, u)
                    if more:
                        layer1(t1 + L1_TILES * (i + 1))
                    else:
                        residual(nb + 2 * i, 8 * i, 0)
                        if into_att:
                            for u in range(3, 5):
                                max_unit(0, 0, u)
                        residual(nb + 2 * i + 1, 8 * i + 4, 1)

                if f == 0:
                    dve.wait_ge(x_in, 16)
                    for step in norm_steps(n0, 0):
                        step()
                    weight_lo(0)
                    weight_lo(1)
                    normalise(n0, 0, 0)
                    normalise(n0, 4, 4)
                    low_x(nb, 0)
                    weight_lo_max(0)
                    weight_lo_max(1)
                    low_x(nb + 1, 1)
                    dve.wait_ge(consts_in, 16 * N_CONSTS)
                    D.tensor_scalar(S3H[:, :], S3[:, :], 0.5, None, ALU.mult).then_inc(s3_half, 1)
                    side = {t: lambda k=t + 2: weight_lo_max(k) for t in range(5)}
                    layer1(t1, side | {5: all_lo_max, 6: take_flag})
                    dve.wait_ge(x_rest_in, 16 * (NP - 1))
                    dve.wait_ge(att_in, 16 * N_ATT_CONSTS)
                else:
                    b = NBATCH - 1
                    layer1(t1, {0: lambda: norm_o(b), 1: lambda: scale_o(b), 5: lambda: add_att(b, 2 * b)})
                    dve.wait_ge(bias_added, NBATCH)
                body(0, first=True)
                with dve.Fori(1, NP - 1) as i:
                    body(i)
                body(NP - 1, more=False)

            ffn_phase(0)

            def attend(b, bb, prev=True, prev2=True, more=True, steps=(), norm=None, ahead=None, v_pair=None):
                for u in range(UNITS):
                    if more:
                        max_unit(b + 1, 1 - bb, u)
                    if u == 2:
                        if prev2:
                            add_att(b - 2, 2 * b - 4)
                        low_max(b)
                    if u == 3 and norm is not None:
                        n, tile0, width = norm
                        normalise(n, tile0, 0)
                        if width > 4:
                            normalise(n, tile0 + 4, 4)
                    if u == 5 and v_pair is not None:
                        set_v(*v_pair)
                    if u == 8 and ahead is not None:
                        low_qk(ahead, 0)
                    if u == 9 and ahead is not None:
                        low_qk(ahead, 2)
                    if u >= 7:
                        for step in steps[u - 7:u - 6]:
                            step()
                    if u == SKEW + 4 and prev:
                        norm_o(b - 1)
                    if u == SKEW + 5 and prev:
                        scale_o(b - 1)

            for u in range(5, UNITS):
                max_unit(0, 0, u)
                if u == 12:
                    low_qk(1, 0)
            low_qk(1, 2)

            def att_body(i, par, ahead=True, more=True, first=False):
                if ahead:
                    q = i + 2
                    steps, norm = norm_steps(norm_of(q), 4 * q, 4), (norm_of(q), 4 * q, 4)
                elif not more:
                    steps, norm = norm_steps(NORMS1, 0, biased=4), (NORMS1, 0, 8)
                else:
                    steps, norm = (), None
                attend(2 * i, 0, prev=not first, prev2=not first, steps=steps)
                attend(2 * i + 1, 1, prev2=not first, more=more, norm=norm, ahead=i + 2 if ahead else None,
                       v_pair=(i + 1, 1 - par) if more else None)

            att_body(0, 0, first=True)
            att_body(1, 1)
            with dve.Fori(1, NPAIR // 2 - 1) as n:
                att_body(2 * n, 0)
                att_body(2 * n + 1, 1)
            att_body(NPAIR - 2, 0, ahead=False)
            att_body(NPAIR - 1, 1, ahead=False, more=False)
            add_att(NBATCH - 2, 2 * NBATCH - 4)
            low_x(NB, 0)
            low_x(NB + 1, 1)
            ffn_phase(1)

        @block.tensor
        def _(pe):
            T = nc.tensor
            T.sem_inc(pv_mm, CREDIT)
            MM = T.matmul

            def split_mm(dst, w, xs, general):
                todo = [(wh, part) for (wh, _), (xh, xl) in zip(w, xs) for part in (xh, xl)]
                if general:
                    todo += [(wl, part) for (_, wl), (xh, xl) in zip(w, xs) for part in (xh, xl)]
                for k, (a, b) in enumerate(todo):
                    ins = MM(dst, a, b, start=k == 0, stop=k == len(todo) - 1)
                return ins

            def w_of(c, t):
                return WH[:, c, P * t:P * t + P], WL[:, c, P * t:P * t + P]

            def layer1(n0, nblk, general, between={}):
                for t in range(L1_TILES):
                    j, n = t // HT, n0 + t
                    if t % HT == 0:
                        pe.wait_ge(xlo_done, nblk + j + 1)
                    xs = [(x_hi[:, j, :], x_lo[:, j, :])]
                    last = n - 3 if t >= 3 else n - 2
                    if t != 2:
                        wait(pe, silu_done, last + 1)
                    split_mm(bank[GATE_BANKS[t]][:, :], [w_of(C_W1, t % HT)], xs, general).then_inc(gate_mm, 1)
                    if t != 2:
                        wait(pe, h_full, last + 1)
                    split_mm(bank[UP_BANKS[t]][:, :], [w_of(C_W2, t % HT)], xs, general).then_inc(up_mm, 1)
                    if t in between:
                        between[t]()

            def inputs_of(layer, j):
                return [(act_hi[layer][:, j, k, :], act_lo[layer][:, j, k, :]) for k in range(HT)]

            def hidden(n0, layer, j, ready_sem, ready, general, between={}):
                pe.wait_ge(ready_sem, ready)
                xs = inputs_of(layer, j)
                c0 = (C_H1, C_H2)[layer]
                for t in range(HT):
                    pe.wait_ge(g_hi, n0 + t + 1)
                    split_mm(bank[4 + t % 2][:, :], [w_of(c0 + k, t) for k in range(HT)], xs, general)\
                        .then_inc(hid_mm, 1)
                    if t in between:
                        between[t]()

            def output(nblk, j, g_ready, general):
                pe.wait_ge(g_lo, g_ready + SLOTS)
                split_mm(bank[6 + j][:, :], [w_of(C_W3, k) for k in range(HT)], inputs_of(2, j), general)\
                    .then_inc(out_mm, 1)

            def transpose_x(nx, j):
                pe.wait_ge(xn_done, nx + 1)
                for t in range(TT):
                    ins = T.transpose(bank[6 + j][:, P * t:P * t + P], xn[:, 4 * j + t, :], EYE[:, :])
                ins.then_inc(xT_done, 1)

            def transpose_y(nblk, j):
                pe.wait_ge(y_scaled, nblk + 1)
                for t in range(TT):
                    ins = T.transpose(bank[6 + j][:, P * t:P * t + P], yT[:, j, P * t:P * t + P], EYE[:, :])
                ins.then_inc(y_back, 1)

            def transpose_att(q, t0):
                pe.wait_ge(xn_done, NB + q + 1)
                for t in range(TT):
                    ins = T.transpose(bank[6][:, P * t:P * t + P], xn[:, t0 + t, :], EYE[:, :])
                ins.then_inc(a_xT, 1)

            def project_q(q):
                pe.wait_ge(a_xT_sb, q + 1)
                MM(bank[7][:, :], WA[:, 0, :], xT[:, :], start=True, stop=True).then_inc(q_mm, 1)

            def project_k(q):
                pe.wait_ge(a_xT_sb, q + 1)
                MM(bank[6][:, :], WA[:, 1, :], xT[:, :], start=True, stop=True).then_inc(k_mm, 1)

            def project_v(q):
                for t in range(TT):
                    ins = MM(bank[7][:, P * t:P * t + P], xT[:, P * t:P * t + P], WA[:, 2, :],
                             start=True, stop=True)
                ins.then_inc(v_mm, 1)

            def max_scores(b, par, bb, u):
                qt, j, s = a_unit(u)
                ahead = next(d for d in range(1, UNITS) if A_BANKS[u - d] == A_BANKS[u])
                wait(pe, max_done, UNITS * b + u - ahead + 1)
                for i in range(2):
                    ins = MM(bank[A_BANKS[u]][:, SEQ * i:SEQ * i + SEQ],
                             QA[par][:, bb, 2 * j + i, P * qt:P * qt + P],
                             KA[par][:, s, bb, 2 * j + i, :], start=True, stop=True)
                ins.then_inc(a_mm, 1)

            def scores(b, par, bb, v):
                j, kt, s = b_unit(v)
                pe.wait_ge(exp_done, UNITS * b + v - 1 + CREDIT)
                for i in range(2):
                    ins = MM(bank[2 + v % 2][:, SEQ * i:SEQ * i + SEQ],
                             KA[par][:, s, bb, 2 * j + i, P * kt:P * kt + P],
                             QA[par][:, bb, 2 * j + i, :], start=True, stop=True)
                ins.then_inc(b_mm, 1)

            def weigh(b, par, bb, g, kt):
                pe.wait_ge(exp_done, UNITS * b + 4 * g + 2 * kt + 2 + CREDIT)
                if kt == 0 and g % 2 == 0:
                    wait(pe, o_out, 2 * b + g // 2)
                for h in range(4):
                    col = VW * (4 * g + h)
                    ins = MM(bank[4][32 * h:32 * h + 32, SEQ * (g % 2):SEQ * (g % 2) + SEQ],
                             V[par][:, 2 * bb + kt, col:col + 32],
                             probs[:, (4 * g + 2 * kt + h % 2) % 8, SEQ * (h // 2):SEQ * (h // 2) + SEQ],
                             start=kt == 0, stop=kt == 1, tile_position=(0, 32 * h))
                if kt == 1:
                    ins.then_inc(pv_mm, 1)

            def max_rows(b, bb):
                pe.wait_ge(max_done, UNITS * b + UNITS)
                for qt in range(2):
                    ins = T.transpose(bank[6][0:HEADS, P * qt:P * qt + P], neg_max[:, bb, qt, :], EYE[:, :])
                ins.then_inc(m_T, 1)

            def tokens_of_o(b):
                pe.wait_ge(o_out, 2 * b + 2)
                for qt in range(2):
                    for g in range(4):
                        ins = T.transpose(bank[6 + qt][:, P * g:P * g + P], oT[:, g, P * qt:P * qt + P],
                                          EYE[:, :])
                    ins.then_inc(o_tok, 1)

            def transpose_o(b):
                pe.wait_ge(o_norm, 2 * b + 2)
                for qt in range(2):
                    ins = T.transpose(bank[6][:, P * qt:P * qt + P], o_nat[:, qt, :], EYE[:, :])
                ins.then_inc(on_T, 1)

            def project_out(b):
                pe.wait_ge(on_T_sb, b + 1)
                for qt in range(2):
                    dst = bank[7][:, P * qt:P * qt + P]
                    ins = MM(dst, onT[:, P * qt:P * qt + P], WA[:, 3, :], start=True, stop=True)
                ins.then_inc(y_mm, 1)

            def ffn_bodies(f, general):
                t1, t2, nb, nx = f * NB * HT, f * NP * HID_TILES, f * NB, f * XN1

                def body(i, first=False, more=True):
                    g = t2 + HID_TILES * i
                    hl = t1 + L1_TILES * i
                    into_att = f == 0 and not more
                    pe.wait_ge(h_full, hl + 6)
                    hidden(g, 0, 0, h_lo, hl + HT, general)
                    before = nb + 2 * i - 2
                    hidden(g + HT, 0, 1, h_lo, hl + 2 * HT, general,
                           {} if first else {0: lambda: transpose_y(before, 0),
                                             1: lambda: transpose_y(before + 1, 1)})

                    def tokens():
                        pe.wait_ge(x_added, nb + 2 * i + CREDIT)
                        transpose_att(0, 0)
                    hidden(g + 2 * HT, 1, 0, g_lo, g + HT + SLOTS, general, {1: tokens} if into_att else {})
                    if more:
                        for j in range(2):
                            pe.wait_ge(x_added, nb + 2 * i - 1 + j + CREDIT)
                            transpose_x(nx + 2 * i + 2 + j, j)
                    if into_att:
                        project_q(0)
                        project_k(0)
                    hidden(g + 3 * HT, 1, 1, g_lo, g + 2 * HT + SLOTS, general)
                    if more:
                        def output_a():
                            output(nb + 2 * i, 0, g + 3 * HT, general)
                            pe.wait_ge(g_hi, g + 4 * HT + CREDIT)

                        def output_b():
                            pe.wait_ge(xlo_done, nb + 2 * i + 4)
                            output(nb + 2 * i + 1, 1, g + 4 * HT, general)
                        layer1(hl + L1_TILES, nb + 2 * i + 2, general, {1: output_a, 4: output_b})
                    else:
                        if into_att:
                            pe.wait_ge(q_lo, 1)
                            project_v(0)
                            pe.wait_ge(k_lo, 1)
                        else:
                            pe.wait_ge(x_added, nb + 2 * i + CREDIT)
                        output(nb + 2 * i, 0, g + 3 * HT, general)
                        if into_att:
                            pe.wait_ge(v_set, 4 + 1)
                        output(nb + 2 * i + 1, 1, g + 4 * HT, general)
                    if into_att:
                        pe.wait_ge(pads_in[0][0], 64)
                        pe.wait_ge(qk_loaded[0][0], 96)
                        pe.wait_ge(g_hi, NP * HID_TILES + CREDIT)
                        for u in range(3):
                            max_scores(0, 0, 0, u)
                    if not more:
                        transpose_y(nb + 2 * i, 0)
                        if into_att:
                            for u in range(3, 5):
                                max_scores(0, 0, 0, u)
                        transpose_y(nb + 2 * i + 1, 1)

                if f == 1:
                    b = NBATCH - 1
                    def tokens():
                        pe.wait_ge(xlo_done, NB + 2)
                        tokens_of_o(b)
                    layer1(t1, nb, general, {1: tokens, 3: lambda: transpose_o(b), 4: lambda: project_out(b)})
                    pe.wait_ge(att_added, NBATCH)
                body(0, first=True)
                with pe.Fori(1, NP - 1) as i:
                    body(i)
                body(NP - 1, more=False)

            def ffn_phase(f, low_weights):
                if f == 0:
                    pe.wait_ge(eye_in, 16)
                    transpose_x(0, 0)
                    transpose_x(1, 1)
                    pe.wait_ge(w_lo, 2)
                    def sum_low_max():
                        pe.wait_ge(ones_set, 1)
                        pe.wait_ge(lo_reduced, len(W_GROUPS) + 1)
                        MM(bank[6][0:1, 0:1], ONES[:, 0:1], lo_max[:, len(W_GROUPS):len(W_GROUPS) + 1],
                           start=True, stop=True).then_inc(flag_sum, 1)
                    layer1(0, 0, True)
                    sum_low_max()
                    pe.wait_ge(flag_set, 1)
                    pe.reg_load(low_weights, flag[0:1, 0:1].bitcast(I32))
                with pe.If_ne(low_weights, 0):
                    ffn_bodies(f, True)
                with pe.Else():
                    ffn_bodies(f, False)

            low_weights = T.alloc_register("low_weights")
            ffn_phase(0, low_weights)

            def attend(b, pair, par, bb, prev=True, prev2=True, own=True, more=True, steps=UNITS,
                       ahead=None, v_pair=None):
                npar, nbb = (par, 1) if bb == 0 else (1 - par, 0)
                ppar, pbb = (par, 0) if bb == 1 else (1 - par, 1)
                if more:
                    of = pair + 1 - nbb
                    pe.wait_ge(pads_in[npar][nbb], 64)
                    pe.wait_ge(qk_loaded[npar][nbb], 48 * (of - npar) + 96)
                    if nbb == 0 and not (isinstance(pair, int) and pair == 0):
                        pe.wait_ge(qa_cleared, 32 * pair)
                for u in range(steps):
                    if more:
                        max_scores(b + 1, npar, nbb, u)
                    for d, v in in_step(u, prev, own):
                        at = (b - d, par, bb) if d == 0 else (b - d, ppar, pbb)
                        if d == 0 and v == 0:
                            pe.wait_ge(m_loaded, 64 * (b + 1))
                        if v < UNITS:
                            scores(*at, v)
                        if v >= 4 and v % 4 == 0:
                            weigh(*at, v // 4 - 1, 0)
                        if v >= 6 and v % 4 == 2:
                            weigh(*at, v // 4 - 1, 1)
                    if u == 1 and prev2:
                        project_out(b - 2)
                    if u == 1 and own:
                        if not prev2:
                            pe.wait_ge(m_lo, b) if prev else pe.wait_ge(k_lo, 2)
                        max_rows(b, bb)
                    if u == 5 and not own:
                        pe.wait_ge(att_added, b - 1)
                        transpose_x(XN1, 0)
                        transpose_x(XN1 + 1, 1)
                    if u == 4 and v_pair is not None:
                        pe.wait_ge(att_added, b - 1) if prev2 else pe.wait_ge(q_lo, 2)
                        project_v(v_pair)
                    if u == 5 and ahead is not None:
                        pe.wait_ge(m_lo, b + 1)
                        transpose_att(ahead, 0)
                    if u == 7 and ahead is not None:
                        pe.wait_ge(v_set, 4 + v_pair + 1)
                        project_q(ahead)
                    if u == 8 and ahead is not None:
                        project_k(ahead)
                    if u == SKEW + 4 and own and prev:
                        if ahead is not None:
                            pe.wait_ge(k_lo, ahead + 1)
                        else:
                            pe.wait_ge(m_lo, b + 1)
                            if v_pair is not None:
                                pe.wait_ge(v_set, 4 + v_pair + 1)
                        tokens_of_o(b - 1)
                    if u == 15 and own and prev:
                        transpose_o(b - 1)

            for u in range(5, UNITS):
                max_scores(0, 0, 0, u)
                if u == 6:
                    pe.wait_ge(x_added, NB + CREDIT)
                    transpose_att(1, 4)
                if u == 10:
                    project_q(1)
                if u == 13:
                    project_k(1)

            def att_body(i, par, ahead=True, more=True, first=False):
                attend(2 * i, i, par, 0, prev=not first, prev2=not first)
                attend(2 * i + 1, i, par, 1, prev2=not first, more=more, ahead=i + 2 if ahead else None,
                       v_pair=i + 1 if more else None)

            att_body(0, 0, first=True)
            att_body(1, 1)
            with pe.Fori(1, NPAIR // 2 - 1) as n:
                att_body(2 * n, 0)
                att_body(2 * n + 1, 1)
            att_body(NPAIR - 2, 0, ahead=False)
            att_body(NPAIR - 1, 1, ahead=False, more=False)
            attend(NBATCH, NPAIR, 0, 0, own=False, more=False, steps=SKEW + 3)
            ffn_phase(1, low_weights)


def kernel(**inputs):
    import numpy as np
    import concourse.bacc as bacc
    from concourse.bass_utils import run_bass_kernel_spmd

    g = {k.removeprefix("L0_"): np.asarray(v) for k, v in inputs.items()}
    x = g["attn_x"]

    def columns(v):
        return v.reshape(-1, P).T

    def k_major(w):
        return w.T.reshape(-1, P, w.shape[0]).transpose(1, 0, 2)

    def by_pair(v):
        return np.moveaxis(v.reshape(*v.shape[:-1], PAIRS, 2, HD), -3, -1).reshape(v.shape)

    ffn = [k_major(g[n]).reshape(P, -1, 512) for n in ("ffn_w1_w", "ffn_w2_w", "ffn_h1_w", "ffn_h2_w", "ffn_w3_w")]
    arrays = {
        "x": x.reshape(-1, P),
        "w_ffn": np.concatenate(ffn, axis=1),
        "w_att": np.stack([by_pair(g["attn_" + n].T) for n in ("Wq", "Wk")]
                          + [g["attn_" + n].T for n in ("Wv", "Wo")], axis=1),
        "s12": np.stack([columns(g["ffn_w1_s"]), columns(g["ffn_w2_s"])], axis=1),
        "sg": np.stack([columns(g["ffn_h1_s"]), columns(g["ffn_h2_s"])], axis=1),
        "s3": columns(g["ffn_w3_s"]),
        "bqk": np.stack([by_pair(g["attn_bq"]), by_pair(g["attn_bk"])], axis=1),
        "bv": g["attn_bv"],
        "bo": g["attn_bo"],
        "eye": np.eye(P, dtype=np.float32),
    }
    arrays = {k: np.ascontiguousarray(v) for k, v in arrays.items()}
    nc = bacc.Bacc("TRN2", target_bir_lowering=False, num_devices=1)
    args = {k: nc.dram_tensor(k, v.shape, F32, kind="ExternalInput").ap() for k, v in arrays.items()}
    out = nc.dram_tensor("out", arrays["x"].shape, F32, kind="ExternalOutput").ap()
    macaron_kernel(nc, out=out, **args)
    r = run_bass_kernel_spmd(nc, [arrays], core_ids=[0])
    return r.results[0]["out"].reshape(x.shape)
```
